# Optimizing a Trainium2 kernel written in Bass

```python
import numpy as np
import jax
import jax.numpy as jnp

def _softmax(x, axis=-1):
    return jax.nn.softmax(x, axis=axis)

def _gelu(x):
    return jax.nn.gelu(x, approximate=True)

def _silu(x):
    return jax.nn.silu(x)

def _sigmoid(x):
    return jax.nn.sigmoid(x)

def _layernorm(x, axis=-1, eps=1e-05):
    m = jnp.mean(x, axis=axis, keepdims=True)
    v = jnp.var(x, axis=axis, keepdims=True)
    return (x - m) / jnp.sqrt(v + eps)

def _scatter_add(tgt, idx, src, axis=0):
    return tgt.at[idx].add(src)

def _segment_sum(src, seg, n):
    return jax.ops.segment_sum(src, seg, n)
kernel_name = 'mk_conv_attn_hybrid_d2_conv_nhwc128_r4_65f8a1'

def setup_inputs(seed: int=0):
    np.random.seed(seed)
    _w = jnp.asarray

    def _rec_inputs():
        import jax
        import jax.numpy as jnp
        _gk = jax.random.key(seed)
        x = -0.0002928 + 1 * jax.random.normal(jax.random.fold_in(_gk, 1), (8, 16, 16, 32), jnp.float32)
        return x
    x = _rec_inputs()

    def _L0_conv_setup():
        import jax, jax.numpy as jnp
        import numpy as np
        N, H, W, C, G, K = (8, 16, 16, 32, 8, 3)
        GC = C // G
        P = K * K
        PAD = DIL = STRIDE = 1
        OS = 1.0
        EPS = 1e-06
        H_IN, W_IN = (H + 2 * PAD, W + 2 * PAD)

        def _grid_sample_nhwc(img, grid):
            B, Hi, Wi, Cc = img.shape
            gx = (grid[..., 0] + 1.0) * (Wi * 0.5) - 0.5
            gy = (grid[..., 1] + 1.0) * (Hi * 0.5) - 0.5
            x0 = jnp.floor(gx)
            y0 = jnp.floor(gy)
            wx1 = gx - x0
            wy1 = gy - y0
            b = jnp.arange(B).reshape(B, 1, 1)

            def tap(xi, yi, wgt):
                valid = (xi >= 0) & (xi <= Wi - 1) & (yi >= 0) & (yi <= Hi - 1)
                xc = jnp.clip(xi, 0, Wi - 1).astype(jnp.int32)
                yc = jnp.clip(yi, 0, Hi - 1).astype(jnp.int32)
                return img[b, yc, xc] * (wgt * valid)[..., None]
            return tap(x0, y0, (1 - wx1) * (1 - wy1)) + tap(x0 + 1, y0, wx1 * (1 - wy1)) + tap(x0, y0 + 1, (1 - wx1) * wy1) + tap(x0 + 1, y0 + 1, wx1 * wy1)

        def _forward(x, w_in, b_in, dw_w, dw_b, ln_g, ln_b, w_off, b_off, w_msk, b_msk, w_out, b_out):
            n = x.shape[0]
            x_proj = x @ w_in + b_in
            x1 = jax.lax.conv_general_dilated(x, dw_w, (1, 1), [((K - 1) // 2,) * 2] * 2, dimension_numbers=('NHWC', 'HWIO', 'NHWC'), feature_group_count=C) + dw_b
            mu = jnp.mean(x1, -1, keepdims=True)
            var = jnp.mean((x1 - mu) ** 2, -1, keepdims=True)
            x1 = (x1 - mu) * jax.lax.rsqrt(var + EPS) * ln_g + ln_b
            x1 = jax.nn.gelu(x1, approximate=False)
            offset = x1 @ w_off + b_off
            mask = jax.nn.softmax((x1 @ w_msk + b_msk).reshape(n, H, W, G, P), axis=-1)
            ry = (DIL * (K - 1) // 2 + 0.5 + jnp.arange(H, dtype=jnp.float32) * STRIDE) / H_IN
            rx = (DIL * (K - 1) // 2 + 0.5 + jnp.arange(W, dtype=jnp.float32) * STRIDE) / W_IN
            ref = jnp.stack([jnp.broadcast_to(rx[None, :], (H, W)), jnp.broadcast_to(ry[:, None], (H, W))], -1)
            ks = jnp.arange(K, dtype=jnp.float32) * DIL - DIL * (K - 1) // 2
            gxk, gyk = jnp.meshgrid(ks, ks, indexing='ij')
            pts = jnp.stack([gxk / W_IN, gyk / H_IN], -1).reshape(P, 2)
            pts = jnp.tile(pts, (G, 1))
            loc = (ref[:, :, None, :] + pts[None, None, :, :] * OS).reshape(1, H, W, G * P * 2)
            snorm = jnp.tile(jnp.array([W_IN, H_IN], jnp.float32), G * P)
            loc = loc + offset * OS / snorm
            grids = (2.0 * loc - 1.0).reshape(n, H * W, G, P, 2)
            grids = grids.transpose(0, 2, 1, 3, 4).reshape(n * G, H * W, P, 2)
            x_pad = jnp.pad(x_proj, ((0, 0), (PAD, PAD), (PAD, PAD), (0, 0)))
            img = x_pad.reshape(n, H_IN, W_IN, G, GC).transpose(0, 3, 1, 2, 4).reshape(n * G, H_IN, W_IN, GC)
            sampled = _grid_sample_nhwc(img, grids)
            m = mask.reshape(n, H * W, G, P).transpose(0, 2, 1, 3).reshape(n * G, H * W, P)
            out = (sampled * m[..., None]).sum(2)
            out = out.reshape(n, G, H * W, GC).transpose(0, 2, 1, 3).reshape(n, H, W, C)
            return out @ w_out + b_out
        key = jax.random.key(seed)
        k = jax.random.split(key, 8)
        s = 0.02
        f = jnp.float32
        return {'x': jax.random.normal(k[0], (N, H, W, C), f), 'w_in': jax.random.normal(k[1], (C, C), f) * (1.0 / np.sqrt(C)), 'b_in': jnp.zeros((C,), f), 'dw_w': jax.random.normal(k[2], (K, K, 1, C), f) * s, 'dw_b': jnp.zeros((C,), f), 'ln_g': jnp.ones((C,), f), 'ln_b': jnp.zeros((C,), f), 'w_off': jax.random.normal(k[3], (C, G * P * 2), f) * s, 'b_off': jax.random.normal(k[4], (G * P * 2,), f) * s, 'w_msk': jax.random.normal(k[5], (C, G * P), f) * s, 'b_msk': jnp.zeros((G * P,), f), 'w_out': jax.random.normal(k[6], (C, C), f) * (1.0 / np.sqrt(C)), 'b_out': jnp.zeros((C,), f)}
    _L0_conv_all = _L0_conv_setup()
    _L0_conv_in = {k: v for k, v in _L0_conv_all.items() if k in ('w_in', 'b_in', 'dw_w', 'dw_b', 'ln_g', 'ln_b', 'w_off', 'b_off', 'w_msk', 'b_msk', 'w_out', 'b_out')}
    del _L0_conv_all

    def _L1_attn_setup():
        import jax, jax.numpy as jnp
        import numpy as np
        key = jax.random.key(seed)
        x = jax.random.normal(key, (4, 1024, 32), dtype=jnp.float32)
        return {'x': x}
    _L1_attn_all = _L1_attn_setup()
    _L1_attn_in = {k: v for k, v in _L1_attn_all.items() if k in ()}
    del _L1_attn_all

    def _L1_ffn_setup():
        import jax, jax.numpy as jnp
        import numpy as np
        B, N, D, C, E, K = (8, 2048, 32, 32, 8, 2)
        key = jax.random.key(seed)
        k0, k1, k2 = jax.random.split(key, 3)
        x = jax.random.normal(k0, (B, N, D), dtype=jnp.float32)
        router_w = jax.random.normal(k1, (D, E), dtype=jnp.float32) * 0.05
        router_b = jnp.zeros((E,), dtype=jnp.float32)
        expert_w = jax.random.normal(k2, (E, D, C), dtype=jnp.float32) * (1.0 / np.sqrt(D))
        expert_b = jnp.zeros((E, C), dtype=jnp.float32)
        return {'x': x, 'router_w': router_w, 'router_b': router_b, 'expert_w': expert_w, 'expert_b': expert_b}
    _L1_ffn_all = _L1_ffn_setup()
    _L1_ffn_in = {k: v for k, v in _L1_ffn_all.items() if k in ('router_w', 'router_b', 'expert_w', 'expert_b')}
    del _L1_ffn_all
    return {'x': x, 'L0_conv_w_in': _L0_conv_in['w_in'], 'L0_conv_b_in': _L0_conv_in['b_in'], 'L0_conv_dw_w': _L0_conv_in['dw_w'], 'L0_conv_dw_b': _L0_conv_in['dw_b'], 'L0_conv_ln_g': _L0_conv_in['ln_g'], 'L0_conv_ln_b': _L0_conv_in['ln_b'], 'L0_conv_w_off': _L0_conv_in['w_off'], 'L0_conv_b_off': _L0_conv_in['b_off'], 'L0_conv_w_msk': _L0_conv_in['w_msk'], 'L0_conv_b_msk': _L0_conv_in['b_msk'], 'L0_conv_w_out': _L0_conv_in['w_out'], 'L0_conv_b_out': _L0_conv_in['b_out'], 'L1_ffn_router_w': _L1_ffn_in['router_w'], 'L1_ffn_router_b': _L1_ffn_in['router_b'], 'L1_ffn_expert_w': _L1_ffn_in['expert_w'], 'L1_ffn_expert_b': _L1_ffn_in['expert_b']}

def reference(x, L0_conv_w_in, L0_conv_b_in, L0_conv_dw_w, L0_conv_dw_b, L0_conv_ln_g, L0_conv_ln_b, L0_conv_w_off, L0_conv_b_off, L0_conv_w_msk, L0_conv_b_msk, L0_conv_w_out, L0_conv_b_out, L1_ffn_router_w, L1_ffn_router_b, L1_ffn_expert_w, L1_ffn_expert_b):
    import jax
    import jax.numpy as jnp

    def _L0_conv_ref(x, w_in, b_in, dw_w, dw_b, ln_g, ln_b, w_off, b_off, w_msk, b_msk, w_out, b_out):
        import jax, jax.numpy as jnp
        import numpy as np
        N, H, W, C, G, K = (8, 16, 16, 32, 8, 3)
        GC = C // G
        P = K * K
        PAD = DIL = STRIDE = 1
        OS = 1.0
        EPS = 1e-06
        H_IN, W_IN = (H + 2 * PAD, W + 2 * PAD)

        def _grid_sample_nhwc(img, grid):
            B, Hi, Wi, Cc = img.shape
            gx = (grid[..., 0] + 1.0) * (Wi * 0.5) - 0.5
            gy = (grid[..., 1] + 1.0) * (Hi * 0.5) - 0.5
            x0 = jnp.floor(gx)
            y0 = jnp.floor(gy)
            wx1 = gx - x0
            wy1 = gy - y0
            b = jnp.arange(B).reshape(B, 1, 1)

            def tap(xi, yi, wgt):
                valid = (xi >= 0) & (xi <= Wi - 1) & (yi >= 0) & (yi <= Hi - 1)
                xc = jnp.clip(xi, 0, Wi - 1).astype(jnp.int32)
                yc = jnp.clip(yi, 0, Hi - 1).astype(jnp.int32)
                return img[b, yc, xc] * (wgt * valid)[..., None]
            return tap(x0, y0, (1 - wx1) * (1 - wy1)) + tap(x0 + 1, y0, wx1 * (1 - wy1)) + tap(x0, y0 + 1, (1 - wx1) * wy1) + tap(x0 + 1, y0 + 1, wx1 * wy1)

        def _forward(x, w_in, b_in, dw_w, dw_b, ln_g, ln_b, w_off, b_off, w_msk, b_msk, w_out, b_out):
            n = x.shape[0]
            x_proj = x @ w_in + b_in
            x1 = jax.lax.conv_general_dilated(x, dw_w, (1, 1), [((K - 1) // 2,) * 2] * 2, dimension_numbers=('NHWC', 'HWIO', 'NHWC'), feature_group_count=C) + dw_b
            mu = jnp.mean(x1, -1, keepdims=True)
            var = jnp.mean((x1 - mu) ** 2, -1, keepdims=True)
            x1 = (x1 - mu) * jax.lax.rsqrt(var + EPS) * ln_g + ln_b
            x1 = jax.nn.gelu(x1, approximate=False)
            offset = x1 @ w_off + b_off
            mask = jax.nn.softmax((x1 @ w_msk + b_msk).reshape(n, H, W, G, P), axis=-1)
            ry = (DIL * (K - 1) // 2 + 0.5 + jnp.arange(H, dtype=jnp.float32) * STRIDE) / H_IN
            rx = (DIL * (K - 1) // 2 + 0.5 + jnp.arange(W, dtype=jnp.float32) * STRIDE) / W_IN
            ref = jnp.stack([jnp.broadcast_to(rx[None, :], (H, W)), jnp.broadcast_to(ry[:, None], (H, W))], -1)
            ks = jnp.arange(K, dtype=jnp.float32) * DIL - DIL * (K - 1) // 2
            gxk, gyk = jnp.meshgrid(ks, ks, indexing='ij')
            pts = jnp.stack([gxk / W_IN, gyk / H_IN], -1).reshape(P, 2)
            pts = jnp.tile(pts, (G, 1))
            loc = (ref[:, :, None, :] + pts[None, None, :, :] * OS).reshape(1, H, W, G * P * 2)
            snorm = jnp.tile(jnp.array([W_IN, H_IN], jnp.float32), G * P)
            loc = loc + offset * OS / snorm
            grids = (2.0 * loc - 1.0).reshape(n, H * W, G, P, 2)
            grids = grids.transpose(0, 2, 1, 3, 4).reshape(n * G, H * W, P, 2)
            x_pad = jnp.pad(x_proj, ((0, 0), (PAD, PAD), (PAD, PAD), (0, 0)))
            img = x_pad.reshape(n, H_IN, W_IN, G, GC).transpose(0, 3, 1, 2, 4).reshape(n * G, H_IN, W_IN, GC)
            sampled = _grid_sample_nhwc(img, grids)
            m = mask.reshape(n, H * W, G, P).transpose(0, 2, 1, 3).reshape(n * G, H * W, P)
            out = (sampled * m[..., None]).sum(2)
            out = out.reshape(n, G, H * W, GC).transpose(0, 2, 1, 3).reshape(n, H, W, C)
            return out @ w_out + b_out
        return _forward(x, w_in, b_in, dw_w, dw_b, ln_g, ln_b, w_off, b_off, w_msk, b_msk, w_out, b_out)

    def _L1_attn_ref(x):
        import jax, jax.numpy as jnp
        import numpy as np
        scores = jnp.einsum('bsd,btd->bst', x, x)
        attn_weights = jax.nn.softmax(scores, axis=-1)
        return jnp.einsum('bst,btd->bsd', attn_weights, x)

    def _L1_ffn_ref(x, router_w, router_b, expert_w, expert_b):
        import jax, jax.numpy as jnp
        import numpy as np
        B, N, D, C, E, K = (8, 2048, 32, 32, 8, 2)
        router_probs = jax.nn.softmax(x @ router_w + router_b, axis=-1)
        top_p, top_i = jax.lax.top_k(router_probs, K)
        top_p = top_p / jnp.sum(top_p, axis=-1, keepdims=True)
        expert_out = jnp.einsum('bnd,edc->bnec', x, expert_w) + expert_b
        gathered = jnp.take_along_axis(expert_out, top_i[..., None], axis=2)
        return jnp.einsum('bnk,bnkc->bnc', top_p, gathered)

    def _gn(v, G=32, eps=1e-05):
        B_, H_, W_, C_ = v.shape
        g = v.reshape(B_, H_, W_, G, C_ // G)
        m = jnp.mean(g, axis=(1, 2, 4), keepdims=True)
        s = jnp.var(g, axis=(1, 2, 4), keepdims=True)
        return ((g - m) / jnp.sqrt(s + eps)).reshape(v.shape)

    def _ln_c(v, eps=1e-06):
        m = jnp.mean(v, axis=-1, keepdims=True)
        s = jnp.var(v, axis=-1, keepdims=True)
        return (v - m) / jnp.sqrt(s + eps)

    def _ln_t(v, eps=1e-05):
        m = jnp.mean(v, axis=-1, keepdims=True)
        s = jnp.var(v, axis=-1, keepdims=True)
        return (v - m) / jnp.sqrt(s + eps)

    def _to_tokens(v):
        B_, H_, W_, C_ = v.shape
        return v.reshape(B_, H_ * W_, C_)

    def _from_tokens(t, like):
        return t.reshape(like.shape)
    x = x + _L0_conv_ref(_gn(x), L0_conv_w_in, L0_conv_b_in, L0_conv_dw_w, L0_conv_dw_b, L0_conv_ln_g, L0_conv_ln_b, L0_conv_w_off, L0_conv_b_off, L0_conv_w_msk, L0_conv_b_msk, L0_conv_w_out, L0_conv_b_out)
    t = _to_tokens(x)
    t = t + _L1_attn_ref(_ln_t(t))
    t = t + _L1_ffn_ref(_ln_t(t), L1_ffn_router_w, L1_ffn_router_b, L1_ffn_expert_w, L1_ffn_expert_b)
    x = _from_tokens(t, x)
    return x

_drawn_inputs = setup_inputs


def setup_inputs(seed=0):
    import zlib

    import numpy as np

    out = dict(_drawn_inputs(seed))
    spreads = {'L0_conv_b_in': (0.0, 0.1),
     'L0_conv_dw_b': (0.0, 0.1),
     'L0_conv_ln_g': (1.0, 0.2),
     'L0_conv_ln_b': (0.0, 0.36),
     'L0_conv_b_msk': (0.0, 0.1),
     'L0_conv_b_out': (0.0, 0.1),
     'L1_ffn_router_b': (0.0, 0.1),
     'L1_ffn_expert_b': (0.0, 0.1)}
    factors = {}
    for name, (base, spread) in spreads.items():
        noise = np.random.default_rng([zlib.crc32(name.encode()), seed]).standard_normal(out[name].shape)
        drawn = base * np.exp(spread * noise) if base else spread * noise
        out[name] = jnp.asarray(drawn.astype(out[name].dtype))
    for name, factor in factors.items():
        out[name] = (out[name] * factor).astype(out[name].dtype)
    return out
```

```python
from contextlib import ExitStack

import concourse.bass as bass
from concourse import mybir

F32 = mybir.dt.float32
I32 = mybir.dt.int32
ALU = mybir.AluOpType
ACT = mybir.ActivationFunctionType
AX = mybir.AxisListType.X

NI, H, W, C = 8, 16, 16, 32
P = NI * H
G, GC = 8, 4
K = 3
NP = K * K
NOFF, NMSK = 2 * NP * G, NP * G
NPROJ = NOFF + NMSK
PAD = 2 * NI
D = K
TW = 2 * K - 1
XC = 8
NCH = W // XC
XG = XC * G
CH = XC * C
HALVES = 2
NT = NI * HALVES
NE = 8
GN_EPS, CONV_EPS, LN_EPS = 1e-5, 1e-6, 1e-5
SCORE_BOUND = float(C)
MAGIC = 1597463007.0
OUT_OF_RACE = -1e30


def bcast(ap, dim, n):
    shape = list(ap.shape)
    return ap.unsqueeze(dim).to_broadcast(shape[:dim] + [n] + shape[dim:])


def hybrid_block(nc, a, out):
    with ExitStack() as ctx:
        def sb(name, shape, dt=F32):
            return ctx.enter_context(nc.sbuf_tensor(name, shape, dt))

        def sem(name):
            return ctx.enter_context(nc.semaphore(name))

        x_rows = sb("x_rows", [P, W * C])
        x_tok = sb("x_tok", [P, HALVES, NI, C])
        vec_rows = sb("vec_rows", [12, 4, C])
        w_in4 = sb("w_in4", [P, C])
        w_out4 = sb("w_out4", [P, C])
        router4 = sb("router4", [P, NE])
        proj_raw = sb("proj_raw", [97, NPROJ])
        expert4 = sb("expert4", [P, NE, C])
        expert_b16 = sb("expert_b16", [P, C])
        b_in_row = sb("b_in_row", [1, C])
        b_out_all = sb("b_out_all", [P, C])
        router_b_all = sb("router_b_all", [P, NE])
        wide_ident = sb("wide_ident", [P, P + 2 * PAD])
        ident = wide_ident[:, PAD:PAD + P]
        same_image = sb("same_image", [P, NI])
        seg_mean = sb("seg_mean", [P, P])
        quad_mask = sb("quad_mask", [P, 4])
        tile_mask = sb("tile_mask", [P, NT])
        ones = sb("ones", [P, P])
        neg_bound = sb("neg_bound", [P, 1])
        minus_one = sb("minus_one", [P, 1])
        priority = sb("priority", [P, NE])
        centring = sb("centring", [P, C])
        coord_x = sb("coord_x", [P, NCH, NP, XC])
        coord_ky = sb("coord_ky", [P, NP])
        pixel_no = sb("pixel_no", [P, W])
        part_no = sb("part_no", [P, 1], I32)
        vec_cols = sb("vec_cols", [P, 12])
        conv_w = sb("conv_w", [P, K, 6, C])
        conv_bias = sb("conv_bias", [P, P])
        w_in_bd = sb("w_in_bd", [P, 4, C])
        router_bd = sb("router_bd", [P, 4, NE])
        proj_mask = sb("proj_mask", [97, 3])
        proj_w = sb("proj_w", [97, 3, NPROJ])
        expert_b_bd = sb("expert_b_bd", [P, NT, C])
        x_sum = sb("x_sum", [P, C])
        x_cent = sb("x_cent", [P, W * C])
        x_sq = sb("x_sq", [P, W * C])
        x_sqsum = sb("x_sqsum", [P, C])
        gn_rstd = sb("gn_rstd", [P, C])
        xnT = sb("xnT", [P, 4, H + 2, NI])
        x_proj = sb("x_proj", [P, W * C])
        c_sq = sb("c_sq", [P, W * C])
        c_sum = sb("c_sum", [P, W])
        c_rstd = sb("c_rstd", [P, W])
        c_norm = sb("c_norm", [P, W * C])
        gT = sb("gT", [97, 6, P])
        l_max = sb("l_max", [P, NCH, XC, G])
        prob = sb("prob", [P, NCH, NP, XC, G])
        den = sb("den", [P, NCH, XG])
        rden = sb("rden", [P, NCH, XG])
        absoff = sb("absoff", [P, 2 * NP, XG])
        over = sb("over", [P, 2 * NP * XG])
        over_sum = sb("over_sum", [P, NCH])
        over_all = sb("over_all", [P, 1])
        flag = sb("flag", [1, 1], I32)
        hat = sb("hat", [P, NCH, 2 * NP, D, XG])
        my = sb("my", [P, D, NP, XG])
        coef = sb("coef", [P, D, K, TW, XG])
        side1 = sb("side1", [P, D, K, D, XG])
        side2 = sb("side2", [P, D, K, XG])
        taps = sb("taps", [P, 3, TW, CH])
        samp = sb("samp", [P, W * C])
        sampT = sb("sampT", [P, NI, H, 4])
        gen_x = sb("gen_x", [P, NCH, NP, XG])
        gen_y = sb("gen_y", [P, NCH, NP, XG])
        gen_ey = sb("gen_ey", [P, NCH * NP * XG])
        gen_d = absoff[:, :, :].rearrange("p s j -> p (s j)")
        gen_q = over
        gen_a = sb("gen_a", [P, NCH * XG])
        gen_p = c_sq
        gen_acc = x_sq
        gen_ky = sb("gen_ky", [P, NP])
        row_no = sb("row_no", [P, 1], I32)
        row_f = sb("row_f", [P, 1])
        image_all = sb("image_all", [P, H, W * C])
        tok = sb("tok", [P, NT, C])
        tok_s = sb("tok_s", [P, NT])
        tok_c = sb("tok_c", [P, NT, C])
        tok_q = sb("tok_q", [P, NT, C])
        tok_v = sb("tok_v", [P, NT])
        tok_r = sb("tok_r", [P, NT])
        tok_ln = sb("tok_ln", [P, NT, C])
        values = sb("values", [P, NT, C + 1])
        lnT = sb("lnT", [P, 2, HALVES, P])
        probs = image_all[:, 0:H // 2, :].rearrange("p y j -> p (y j)").rearrange(
            "p (n h s) -> p n h s", n=NI, h=HALVES)
        att_r = sb("att_r", [P, NT])
        att = sb("att", [P, NT, C])
        tok2 = sb("tok2", [P, NT, C])
        tok2_ln = sb("tok2_ln", [P, NT, C])
        ln2T = sb("ln2T", [P, 2, HALVES, P])
        logit = sb("logit", [P, NT, NE])
        lsame = sb("lsame", [P, NT, NE])
        first = sb("first", [P, NT, NE])
        second = sb("second", [P, NT, NE])
        l_rest = sb("l_rest", [P, NT, NE])
        top = sb("top", [P, 8, NT])
        gate = sb("gate", [P, NT, NE])
        gateT = sb("gateT", [P, P])
        tok2_b = sb("tok2_b", [P, NT, C])
        gated = sb("gated", [P, 4, NE, C])
        moe = sb("moe", [P, NT, C])
        result = sb("result", [P, NT, C])
        nw = sb("nw", [P, 3, C])

        ps = ctx.enter_context(nc.psum_tensor("ps", [P, 8, 512], F32))
        image_dram = nc.dram_tensor("image_dram", [P, W * C], F32).ap()

        x_in = sem("x_in")
        vec_in = sem("vec_in")
        w_in_in = sem("w_in_in")
        b_in_in = sem("b_in_in")
        proj_in = sem("proj_in")
        tok_in = sem("tok_in")
        late_in = sem("late_in")
        consts = sem("consts")
        pool_step = sem("pool_step")
        w_in_ready = sem("w_in_ready")
        proj_w_ready = sem("proj_w_ready")
        x_tok_ready = sem("x_tok_ready")
        late_ready = sem("late_ready")
        step = sem("step")
        centring_ready = sem("centring_ready")
        vec_T = sem("vec_T")
        conv_w_ready = sem("conv_w_ready")
        x_summed = sem("x_summed")
        x_mean = sem("x_mean")
        x_centred = sem("x_centred")
        x_squared = sem("x_squared")
        x_sqsummed = sem("x_sqsummed")
        x_var = sem("x_var")
        x_normed = sem("x_normed")
        xT_done = sem("xT_done")
        xnT_ready = sem("xnT_ready")
        conv_done = sem("conv_done")
        x_proj_done = sem("x_proj_done")
        x_proj_ready = sem("x_proj_ready")
        conv_squared = sem("conv_squared")
        conv_normed = sem("conv_normed")
        conv_T = sem("conv_T")
        gT_ready = sem("gT_ready")
        proj_done = sem("proj_done")
        logits_read = sem("logits_read")
        probs_ready = sem("probs_ready")
        hats_ready = sem("hats_ready")
        abs_ready = sem("abs_ready")
        over_ready = sem("over_ready")
        over_added = sem("over_added")
        flag_sum = sem("flag_sum")
        flag_ready = sem("flag_ready")
        images_done = sem("images_done")
        taps_ready = sem("taps_ready")
        taps_used = sem("taps_used")
        acc_done = sem("acc_done")
        img_stored = sem("img_stored")
        img_spread = sem("img_spread")
        samp_ready = sem("samp_ready")
        sampT_done = sem("sampT_done")
        sampT_ready = sem("sampT_ready")
        conv_out = sem("conv_out")
        tok_centred = sem("tok_centred")
        tok_squared = sem("tok_squared")
        tok_normed = sem("tok_normed")
        lnT_done = sem("lnT_done")
        lnT_ready = sem("lnT_ready")
        values_ready = sem("values_ready")
        scores_done = sem("scores_done")
        exp_done = sem("exp_done")
        pv_done = sem("pv_done")
        logits_done = sem("logits_done")
        gap_ready = sem("gap_ready")
        gap_exp = sem("gap_exp")
        gate_ready = sem("gate_ready")
        gateT_done = sem("gateT_done")
        gateT_ready = sem("gateT_ready")
        bias_done = sem("bias_done")
        bias_read = sem("bias_read")
        experts_done = sem("experts_done")
        experts_read = sem("experts_read")
        result_ready = sem("result_ready")
        stored = sem("stored")

        block = ctx.enter_context(nc.Block())

        def pbank(b, n=512, at=0):
            return ps[:, b, at:at + n]

        proj_ps = ps[:, :, :].rearrange("p b (t j) -> p (b t) j", t=2)
        CHUNK_SLOT = [8, 0]
        IMG0 = 3
        image_flat = image_all[:, :, :].rearrange("p y j -> p (y j)")
        tok_dram = [[t.rearrange("n y (b q) c -> q (y b) n c", q=4) for t in (a["x"], out)][i] for i in range(2)]

        def window(ch):
            full = [0, 1, 2] if ch == 0 else [0, -1, -2]
            part = [-1, -2] if ch == 0 else [1, 2]
            return [(s, 0, XC) for s in full] + [(s, max(0, -s), XC - max(0, s)) for s in part]

        SCORE_BANK = [5, 6, 7, 0]
        ROW_OF = [0, 1, 2, 5, 8]

        @block.sync
        def _(sp):
            sp.dma_start(x_rows[:, :], a["x"].rearrange("n y x c -> y n (x c)")).then_inc(x_in, 16)
            for dx in range(K):
                r = (K - 1 - dx) * K
                sp.dma_start(vec_rows[r:r + K, :, :],
                             bcast(a["dw_w"][:, dx, 0, :], 1, 4)).then_inc(vec_in, 16)
            sp.dma_start(w_in4[:, :], a["w_in"].unsqueeze(0).to_broadcast([4, C, C])).then_inc(w_in_in, 16)
            sp.dma_start(proj_raw[0:96, 0:NOFF], a["w_off"].unsqueeze(0).to_broadcast([3, C, NOFF])).then_inc(proj_in, 16)
            sp.dma_start(proj_raw[0:96, NOFF:NPROJ], a["w_msk"].unsqueeze(0).to_broadcast([3, C, NMSK])).then_inc(proj_in, 16)
            sp.dma_start(proj_raw[96:97, 0:NOFF], a["b_off"].unsqueeze(0)).then_inc(proj_in, 16)
            sp.dma_start(proj_raw[96:97, NOFF:NPROJ], a["b_msk"].unsqueeze(0)).then_inc(proj_in, 16)
            for q in range(4):
                sp.dma_start(expert4[q * C:(q + 1) * C, :, :],
                             a["expert_w"].rearrange("e d c -> d e c")).then_inc(late_in, 16)
            sp.dma_start(expert_b16[:, :], a["expert_b"].unsqueeze(0).to_broadcast([NT, NE, C])).then_inc(late_in, 16)
            sp.dma_start(router4[:, :], a["router_w"].unsqueeze(0).to_broadcast([4, C, NE])).then_inc(late_in, 16)
            sp.dma_start(w_out4[:, :], a["w_out"].unsqueeze(0).to_broadcast([4, C, C])).then_inc(late_in, 16)
            sp.dma_start(router_b_all[:, :], a["router_b"].unsqueeze(0).to_broadcast([P, NE])).then_inc(late_in, 16)

            sp.wait_ge(flag_ready, 1)
            far = sp.value_load(flag[0:1, 0:1], min_val=0, max_val=1)
            with sp.If(far > 0):
                sp.wait_ge(x_proj_ready, 1)
                sp.dma_start(image_dram, x_proj[:, :]).then_inc(img_stored, 16)
                sp.wait_ge(img_stored, 16)
                for n in range(NI):
                    sp.dma_start(image_all[n:P:NI, :, :],
                                 image_dram[n:P:NI, :].unsqueeze(0).to_broadcast([H, H, W * C])
                                 ).then_inc(img_spread, 16)
            sp.wait_ge(result_ready, 1)
            for q in range(4):
                sp.dma_start(tok_dram[1][q],
                             result[64 * (q % 2):64 * (q % 2) + 64, 8 * (q // 2):8 * (q // 2) + 8, :]
                             ).then_inc(stored, 16)
            sp.wait_ge(stored, 4 * 16)

        @block.gpsimd
        def _(g):
            count = [0]

            def then(ins):
                count[0] += 1
                ins.then_inc(pool_step, 1)
                g.wait_ge(pool_step, count[0])

            def where(view, pattern, base, mult, op, fill):
                return g.affine_select(out=view, in_=view, compare_op=op, fill=fill, base=base,
                                       pattern=pattern, channel_multiplier=mult)

            g.memset(ones[:, :], 1.0)
            g.memset(xnT[:, :, :, :], 0.0)
            then(g.memset(wide_ident[:, :], 0.0))
            where(wide_ident[:, :], [[-1, P + 2 * PAD]], PAD, 1, ALU.not_equal, 1.0).then_inc(consts, 1)
            then(g.memset(quad_mask[:, :], 1.0))
            then(where(quad_mask[:, :], [[-32, 4]], 0, 1, ALU.is_ge, 0.0))
            then(where(quad_mask[:, :], [[32, 4]], 31, -1, ALU.is_ge, 0.0))
            g.memset(neg_bound[:, :], -SCORE_BOUND)
            g.memset(minus_one[:, :], -1.0)
            then(g.memset(conv_w[:, :, :, :], 0.0))
            then(g.memset(gT[:, 5, :], 0.0))
            then(g.memset(gT[96:97, :, :], 1.0))
            g.memset(values[:, :, C:C + 1], 1.0).then_inc(consts, 1)
            g.wait_ge(w_in_in, 16)
            g.tensor_tensor(w_in_bd[:, :, :], bcast(w_in4[:, :], 1, 4), bcast(quad_mask[:, :], 2, C),
                            ALU.mult).then_inc(w_in_ready, 1)
            then(g.tensor_tensor(proj_mask[:, :], quad_mask[0:97, 0:3],
                                 quad_mask[0:97, 3:4].to_broadcast([97, 3]), ALU.add))
            g.wait_ge(proj_in, 4 * 16)
            for q in range(3):
                g.tensor_scalar(proj_w[:, q, 0:NOFF].rearrange("p (t s g) -> p t s g", t=2, g=G),
                                proj_raw[:, 0:NOFF].rearrange("p (g s t) -> p t s g", g=G, t=2),
                                proj_mask[:, q:q + 1], None, ALU.mult)
                ins = g.tensor_scalar(proj_w[:, q, NOFF:NPROJ].rearrange("p (s g) -> p s g", g=G),
                                      proj_raw[:, NOFF:NPROJ].rearrange("p (g s) -> p s g", g=G),
                                      proj_mask[:, q:q + 1], None, ALU.mult)
            ins.then_inc(proj_w_ready, 1)
            g.wait_ge(tok_in, 5 * 16)
            xt = x_tok[:, :, :, :].rearrange("p h n c -> p (h n) c")
            g.tensor_tensor(xt, xt, bcast(b_out_all[:, :], 1, NT), ALU.add).then_inc(x_tok_ready, 1)
            g.wait_ge(late_in, 8 * 16)
            g.tensor_tensor(router_bd[:, :, :], bcast(router4[:, :], 1, 4), bcast(quad_mask[:, :], 2, NE),
                            ALU.mult).then_inc(late_ready, 1)
            then(g.memset(tile_mask[:, :], 1.0))
            then(where(tile_mask[:, :], [[-NE, NT]], 0, 1, ALU.is_ge, 0.0))
            then(where(tile_mask[:, :], [[NE, NT]], NE - 1, -1, ALU.is_ge, 0.0))
            g.tensor_tensor(expert_b_bd[:, :, :], bcast(expert_b16[:, :], 1, NT),
                            bcast(tile_mask[:, :], 2, C), ALU.mult).then_inc(late_ready, 1)
            g.iota(priority[:, :], [[-1, NE]], base=NE, channel_multiplier=0,
                   allow_small_or_imprecise_dtypes=True)
            for ch in range(NCH):
                g.iota(coord_x[:, ch, :, :], [[1, K], [0, K], [1, XC]], base=ch * XC - 1, channel_multiplier=0,
                       allow_small_or_imprecise_dtypes=True)
            g.iota(coord_ky[:, :], [[0, K], [1, K]], base=-1, channel_multiplier=0,
                   allow_small_or_imprecise_dtypes=True)
            g.iota(part_no[:, :], [[0, 1]], base=0, channel_multiplier=1)
            g.iota(pixel_no[:, :], [[1, W]], base=0, channel_multiplier=0,
                   allow_small_or_imprecise_dtypes=True).then_inc(late_ready, 1)

        @block.tensor
        def _(pe):
            pe.wait_ge(consts, 1)
            pe.wait_ge(vec_in, 6 * 16)
            pe.transpose(pbank(0, 12, 128), vec_rows[:, :, :].rearrange("r q c -> r (q c)"),
                         ident[0:12, 0:12]).then_inc(vec_T, 1)
            pe.wait_ge(x_summed, 1)
            pe.wait_ge(conv_w_ready, 1)
            pe.matmul(pbank(0, C), seg_mean[:, :], x_sum[:, :], start=True, stop=True).then_inc(x_mean, 1)
            pe.wait_ge(x_sqsummed, 1)
            pe.matmul(pbank(0, C), seg_mean[:, :], x_sqsum[:, :], start=True, stop=True).then_inc(x_var, 1)
            pe.wait_ge(x_normed, 1)
            for b in range(4):
                ins = pe.transpose(pbank(1, P, b * P), x_rows[:, b * P:(b + 1) * P], ident)
            ins.then_inc(xT_done, 1)
            pe.matmul(pbank(2), conv_bias[:, :], bcast(centring[:, :], 1, W), start=True, stop=False,
                      skip_group_check=True)
            pe.wait_ge(xnT_ready, 1)
            for b in range(4):
                lo, hi = (1, 6) if b == 0 else (0, 5) if b == 3 else (0, 6)
                x0 = 4 * b - 1 + lo
                for dy in range(K):
                    ins = pe.matmul(pbank(2, (hi - lo) * C, x0 * C),
                                    xnT[:, b, dy:dy + H, :], conv_w[:, dy, lo:hi, :],
                                    start=False, stop=(b == 3 and dy == K - 1), skip_group_check=True)
            ins.then_inc(conv_done, 1)
            pe.wait_ge(b_in_in, 16)
            pe.wait_ge(w_in_ready, 1)
            pe.matmul(pbank(3), ones[0:1, :], bcast(b_in_row[:, :], 1, W), start=True, stop=False,
                      skip_group_check=True)
            for b in range(4):
                ins = pe.matmul(pbank(3, P, b * P), xnT[:, b, 1:1 + H, :], w_in_bd[:, :, :],
                                start=False, stop=(b == 3), skip_group_check=True)
            ins.then_inc(x_proj_done, 1)
            pe.wait_ge(conv_normed, 1)
            for t in range(6):
                n = min(3, W - 3 * t) * C
                ins = pe.transpose(ps[0:n, t // 4, (t % 4) * P:(t % 4 + 1) * P],
                                   c_norm[:, 3 * C * t:3 * C * t + n], ident)
            ins.then_inc(conv_T, 1)
            pe.wait_ge(proj_w_ready, 1)
            pe.wait_ge(gT_ready, 1)
            for ch in range(NCH):
                if ch == 1:
                    pe.wait_ge(x_proj_ready, 1)
                for i in range(XC):
                    x = ch * XC + i
                    ins = pe.matmul(proj_ps[:, CHUNK_SLOT[ch] + i, 0:NPROJ], gT[:, x // 3, :],
                                    proj_w[:, x % 3, :], start=True, stop=True)
                ins.then_inc(proj_done, 1)
            pe.wait_ge(over_ready, 2)
            pe.wait_ge(logits_read, 2)
            for dy in (0, -1, 1, -2, 2):
                pe.matmul(pbank(IMG0 + 2 + dy), wide_ident[:, PAD + NI * dy:PAD + NI * dy + P], x_proj[:, :], start=True, stop=True).then_inc(images_done, 1)
            pe.wait_ge(over_added, 1)
            pe.matmul(ps[0:1, 2, 0:1], over_all[:, :], ones[:, 0:1], start=True, stop=True).then_inc(flag_sum, 1)
            for ch in range(NCH):
                for ty in range(TW):
                    pe.wait_ge(taps_ready, ch * TW + ty + 1)
                    for j, (s, lo, hi) in enumerate(window(ch)):
                        ins = pe.matmul(pbank(ch, (hi - lo) * C, lo * C), ident,
                                        taps[:, (ch * TW + ty) % 3, s + 2, lo * C:hi * C],
                                        start=(ty == 0 and j == 0), stop=(ty == TW - 1 and j == TW - 1),
                                        skip_group_check=True)
                    ins.then_inc(taps_used, 1)
            pe.wait_ge(samp_ready, 1)
            pe.wait_ge(flag_ready, 1)
            for b in range(4):
                ins = pe.transpose(pbank(2, P, b * P), samp[:, b * P:(b + 1) * P], ident)
            ins.then_inc(sampT_done, 1)
            pe.wait_ge(sampT_ready, 1)
            pe.wait_ge(late_in, 8 * 16)
            for q in range(4):
                for n in range(NI):
                    ins = pe.matmul(ps[64 * (q % 2):64 * (q % 2) + 64, 3 + q // 2, n * C:(n + 1) * C],
                                    sampT[q * C:(q + 1) * C, n, :, :], w_out4[q * C:(q + 1) * C, :],
                                    start=True, stop=True)
            ins.then_inc(conv_out, 1)

            def channels_first(dst_bank, src):
                for n2 in range(2):
                    for h in range(HALVES):
                        i = h * NI + n2 * 4
                        t = pe.transpose(pbank(dst_bank, P, (n2 * HALVES + h) * P), src[:, i:i + 4, :],
                                         ident)
                return t

            pe.wait_ge(tok_normed, 1)
            channels_first(2, tok_ln).then_inc(lnT_done, 1)
            pe.wait_ge(lnT_ready, 1)

            def scores(n):
                q, n2 = n % 4, n // 4
                for h in range(HALVES):
                    ins = pe.matmul(pbank(SCORE_BANK[q], 2 * P, h * 2 * P), lnT[q * C:(q + 1) * C, n2, h, :],
                                    lnT[q * C:(q + 1) * C, n2, :, :], start=True, stop=True)
                ins.then_inc(scores_done, 1)

            def weighted(n):
                pe.wait_ge(exp_done, n + 1)
                for s in range(HALVES):
                    for h in range(HALVES):
                        ins = pe.matmul(pbank(3 + s, C + 1, n * (C + 1)), probs[:, n, h, s * P:(s + 1) * P],
                                        values[:, h * NI + n, :], start=(h == 0), stop=(h == HALVES - 1))
                ins.then_inc(pv_done, 1)

            for n in range(NI):
                if n >= 4:
                    pe.wait_ge(exp_done, n - 3)
                scores(n)
                if n == 2:
                    pe.wait_ge(values_ready, 1)
                if n >= 2:
                    weighted(n - 2)
            weighted(NI - 2)
            weighted(NI - 1)
            pe.wait_ge(tok_normed, 2)
            channels_first(2, tok2_ln).then_inc(lnT_done, 1)
            pe.wait_ge(lnT_ready, 2)
            pe.wait_ge(late_ready, 3)
            for n2 in range(2):
                for h in range(HALVES):
                    ins = pe.matmul(pbank(0, 4 * NE, (h * NI + n2 * 4) * NE), ln2T[:, n2, h, :],
                                    router_bd[:, :, :], start=True, stop=True)
            ins.then_inc(logits_done, 1)

            def experts(k):
                h, n2 = k // 2, k % 2
                for q in range(4):
                    ins = pe.matmul(pbank(4 - 4 * (k % 2) + q, NE * C), ln2T[q * C:(q + 1) * C, n2, h, :],
                                    expert4[q * C:(q + 1) * C, :, :], start=True, stop=True)
                ins.then_inc(experts_done, 1)

            experts(0)
            pe.wait_ge(gate_ready, 1)
            pe.transpose(pbank(1, P), gate[:, :, :], ident).then_inc(gateT_done, 1)
            pe.wait_ge(gateT_ready, 1)
            pe.matmul(pbank(2), gateT[:, :], expert_b_bd[:, :, :], start=True, stop=True).then_inc(bias_done, 1)
            pe.wait_ge(bias_read, 1)
            experts(1)
            pe.wait_ge(experts_read, 1)
            experts(2)
            pe.wait_ge(experts_read, 2)
            experts(3)

        @block.scalar
        def _(act):
            for i, name in enumerate(("dw_b", "ln_g", "ln_b")):
                act.dma_start(vec_rows[NP + i:NP + i + 1, :, :],
                              a[name].unsqueeze(0).unsqueeze(0).to_broadcast([1, 4, C])).then_inc(vec_in, 16)
            act.dma_start(b_in_row[:, :], a["b_in"].unsqueeze(0)).then_inc(b_in_in, 16)
            for q in range(4):
                act.dma_start(x_tok[64 * (q % 2):64 * (q % 2) + 64, q // 2, :, :], tok_dram[0][q]).then_inc(tok_in, 16)
            act.dma_start(b_out_all[:, :], a["b_out"].unsqueeze(0).to_broadcast([P, C])).then_inc(tok_in, 16)
            act.wait_ge(x_centred, 1)
            act.activation(x_sq[:, :], x_cent[:, :], ACT.Square).then_inc(x_squared, 1)
            act.wait_ge(conv_done, 1)
            act.activation(c_sq[:, :], pbank(2), ACT.Square).then_inc(conv_squared, 1)
            act.wait_ge(x_proj_done, 1)
            act.activation(x_proj[:, :], pbank(3), ACT.Copy).then_inc(x_proj_ready, 1)
            act.wait_ge(consts, 2)
            act.wait_ge(conv_T, 1)
            act.activation(gT[0:96, 0:5, :], ps[0:96, 0:2, :].rearrange("p b j -> p (b j)")[:, 0:5 * P].rearrange("p (t j) -> p t j", j=P),
                           ACT.Gelu, bias=vec_cols[0:96, 11:12], scale=vec_cols[0:96, 10:11])
            act.activation(gT[0:32, 5, :], ps[0:32, 1, P:2 * P], ACT.Gelu, bias=vec_cols[0:32, 11:12],
                           scale=vec_cols[0:32, 10:11]).then_inc(gT_ready, 1)
            for ch in range(NCH):
                slot = CHUNK_SLOT[ch]
                act.wait_ge(logits_read, ch + 1)
                if ch > 0:
                    act.wait_ge(over_ready, ch)
                flat = proj_ps[:, slot:slot + XC, 0:NOFF].rearrange("p x (s g) -> p x s g", g=G)
                hx = hat[:, ch, :, :, :].rearrange("p s d (x g) -> p d x s g", g=G)
                ab = absoff[:, :, :].rearrange("p s (x g) -> p x s g", g=G)
                act.activation(prob[:, ch, :, :, :], prob[:, ch, :, :, :], ACT.Exp).then_inc(probs_ready, 1)
                act.activation(ab, flat, ACT.Abs).then_inc(abs_ready, 1)
                act.activation(hx[:, 0], flat, ACT.Relu, scale=-1.0)
                act.activation(hx[:, 2], flat, ACT.Relu)
                act.wait_ge(abs_ready, ch + 1)
                act.activation(hat[:, ch, :, 1, :], absoff[:, :, :], ACT.Copy, bias=1.0, scale=-1.0).then_inc(hats_ready, 1)
                act.activation(over[:, :], absoff[:, :, :].rearrange("p s j -> p (s j)"), ACT.Relu, bias=minus_one[:, :],
                               accum_out=over_sum[:, ch:ch + 1]).then_inc(over_ready, 1)
            act.wait_ge(sampT_done, 1)
            act.activation(sampT[:, :, :, :].rearrange("p n y b -> p b y n"),
                           pbank(2).rearrange("p (b y n) -> p b y n", b=4, n=NI), ACT.Copy).then_inc(sampT_ready, 1)
            act.wait_ge(tok_centred, 1)
            act.activation(tok_q[:, :, :], tok_c[:, :, :], ACT.Square).then_inc(tok_squared, 1)
            act.wait_ge(lnT_done, 1)
            act.activation(lnT[:, :, :, :].rearrange("p a h t -> p (a h t)"), pbank(2), ACT.Copy).then_inc(lnT_ready, 1)
            act.activation(values[:, :, 0:C], tok_ln[:, :, :], ACT.Copy).then_inc(values_ready, 1)
            for n in range(NI):
                act.wait_ge(scores_done, n + 1)
                act.activation(probs[:, n, :, :].rearrange("p h s -> p (h s)"), pbank(SCORE_BANK[n % 4]), ACT.Exp,
                               bias=neg_bound[:, :]).then_inc(exp_done, 1)
            act.wait_ge(tok_centred, 2)
            act.activation(tok_q[:, :, :], tok_c[:, :, :], ACT.Square).then_inc(tok_squared, 1)
            act.wait_ge(lnT_done, 2)
            act.activation(ln2T[:, :, :, :].rearrange("p a h t -> p (a h t)"), pbank(2), ACT.Copy).then_inc(lnT_ready, 1)
            act.wait_ge(gap_ready, 1)
            act.activation(top[:, 4, :], top[:, 3, :], ACT.Exp).then_inc(gap_exp, 1)
            act.wait_ge(gateT_done, 1)
            act.activation(gateT[:, :], pbank(1, P), ACT.Copy).then_inc(gateT_ready, 1)

        @block.vector
        def _(v):
            count = [0]

            def then(ins):
                count[0] += 1
                ins.then_inc(step, 1)
                v.wait_ge(step, count[0])

            def inv_sqrt(dst, src, scale, eps):
                n = dst.shape[1]
                var, y, t = nw[:, 0, 0:n], dst, nw[:, 1, 0:n]
                then(v.tensor_scalar(var, src, scale, eps, ALU.mult, ALU.add))
                then(v.tensor_scalar(t.bitcast(I32), var.bitcast(I32), 1, None, ALU.logical_shift_right))
                then(v.tensor_scalar(y.bitcast(I32), t.bitcast(I32), -1.0, MAGIC, ALU.mult, ALU.add))
                for _ in range(3):
                    then(v.scalar_tensor_tensor(out=t, in0=y, scalar=-0.5, in1=y, op0=ALU.mult, op1=ALU.mult))
                    then(v.tensor_tensor(t, t, var, ALU.mult))
                    then(v.scalar_tensor_tensor(out=y, in0=t, scalar=1.5, in1=y, op0=ALU.add, op1=ALU.mult))

            v.wait_ge(consts, 1)
            then(v.tensor_reduce(same_image[:, :], ident.rearrange("p (y n) -> p n y", n=NI), AX, ALU.add))
            v.tensor_scalar(seg_mean[:, :].rearrange("p (y n) -> p y n", n=NI), bcast(same_image[:, :], 1, H),
                            1.0 / (H * W), None, ALU.mult)
            then(v.tensor_reduce(centring[:, :], ident.rearrange("p (q c) -> p c q", c=C), AX, ALU.add))
            then(v.tensor_scalar(centring[:, :], centring[:, :], -1.0 / C, None, ALU.add))
            v.wait_ge(vec_T, 1)
            then(v.tensor_copy(vec_cols[:, :], pbank(0, 12, 128)))
            v.wait_ge(consts, 2)
            taps_c = vec_cols[:, 0:NP].rearrange("p (s d) -> p d s", s=K)
            for xi in range(4):
                q = slice(32 * xi, 32 * xi + 32)
                v.tensor_tensor(conv_w[q, :, xi:xi + K, :],
                                centring[q, :].unsqueeze(1).unsqueeze(1).to_broadcast([32, K, K, C]),
                                bcast(taps_c[q, :, :], 3, C), ALU.mult)
            v.tensor_scalar(conv_bias[:, :], ones[:, :], vec_cols[:, 9:10], 0.25, ALU.mult,
                            ALU.mult).then_inc(conv_w_ready, 1)
            v.wait_ge(x_in, 16)
            v.tensor_reduce(x_sum[:, :], x_rows[:, :].rearrange("p (x c) -> p c x", c=C), AX,
                            ALU.add).then_inc(x_summed, 1)
            v.wait_ge(x_mean, 1)
            xr = x_rows[:, :].rearrange("p (x c) -> p x c", c=C)
            xc = x_cent[:, :].rearrange("p (x c) -> p x c", c=C)
            v.tensor_tensor(xc, xr, bcast(pbank(0, C), 1, W), ALU.subtract).then_inc(x_centred, 1)
            v.wait_ge(x_squared, 1)
            v.tensor_reduce(x_sqsum[:, :], x_sq[:, :].rearrange("p (x c) -> p c x", c=C), AX,
                            ALU.add).then_inc(x_sqsummed, 1)
            v.wait_ge(x_var, 1)
            inv_sqrt(gn_rstd[:, :], pbank(0, C), 1.0, GN_EPS)
            v.tensor_tensor(xr, xc, bcast(gn_rstd[:, :], 1, W), ALU.mult).then_inc(x_normed, 1)
            v.wait_ge(xT_done, 1)
            v.tensor_copy(xnT[:, :, 1:1 + H, :], pbank(1).rearrange("p (b y n) -> p b y n", b=4, n=NI)
                          ).then_inc(xnT_ready, 1)
            v.wait_ge(conv_squared, 1)
            then(v.tensor_reduce(c_sum[:, :], c_sq[:, :].rearrange("p (x c) -> p x c", c=C), AX, ALU.add))
            inv_sqrt(c_rstd[:, :], c_sum[:, :], 1.0 / C, CONV_EPS)
            v.tensor_tensor(c_norm[:, :].rearrange("p (x c) -> p x c", c=C),
                            pbank(2).rearrange("p (x c) -> p x c", c=C), bcast(c_rstd[:, :], 2, C),
                            ALU.mult).then_inc(conv_normed, 1)
            for ch in range(NCH):
                slot = CHUNK_SLOT[ch]
                v.wait_ge(proj_done, ch + 1)
                logits = proj_ps[:, slot:slot + XC, NOFF:NPROJ]
                then(v.tensor_reduce(l_max[:, ch, :, :], logits.rearrange("p x (s g) -> p x g s", g=G), AX, ALU.max))
                v.tensor_tensor(prob[:, ch, :, :, :].rearrange("p s x g -> p x s g"),
                                logits.rearrange("p x (s g) -> p x s g", g=G),
                                bcast(l_max[:, ch, :, :], 2, NP), ALU.subtract).then_inc(logits_read, 1)
            for ch in range(NCH):
                v.wait_ge(probs_ready, ch + 1)
                then(v.tensor_reduce(den[:, ch, :], prob[:, ch, :, :, :].rearrange("p s x g -> p (x g) s"),
                                     AX, ALU.add))
                then(v.reciprocal(rden[:, ch, :], den[:, ch, :]))
                v.wait_ge(hats_ready, ch + 1)
                e = prob[:, ch, :, :, :].rearrange("p s x g -> p s (x g)")
                then(v.tensor_tensor(my[:, :, :, :], bcast(e, 1, D),
                                     hat[:, ch, NP:2 * NP, :, :].rearrange("p s d j -> p d s j"), ALU.mult))
                for dy in range(D):
                    def pair(kx, d0, d1):
                        return (bcast(my[:, dy, kx * K:(kx + 1) * K, :], 2, d1 - d0),
                                hat[:, ch, kx * K:(kx + 1) * K, d0:d1, :])
                    v.tensor_tensor(coef[:, dy, :, 0:3, :], *pair(0, 0, 3), ALU.mult)
                    v.tensor_tensor(side1[:, dy, :, :, :], *pair(1, 0, 3), ALU.mult)
                    v.tensor_tensor(coef[:, dy, :, 3:5, :], *pair(2, 1, 3), ALU.mult)
                    ins = v.tensor_tensor(side2[:, dy, :, :].unsqueeze(2), *pair(2, 0, 1), ALU.mult)
                then(ins)
                rows = coef[:, :, :, :, :].rearrange("p d k t j -> p (d k) t j")
                then(v.tensor_tensor(rows[:, :, 1:4, :], rows[:, :, 1:4, :],
                                     side1[:, :, :, :, :].rearrange("p d k t j -> p (d k) t j"), ALU.add))
                then(v.tensor_tensor(rows[:, :, 2, :], rows[:, :, 2, :],
                                     side2[:, :, :, :].rearrange("p d k j -> p (d k) j"), ALU.add))
                flat_rows = rows.rearrange("p r t j -> p r (t j)")
                then(v.tensor_tensor(flat_rows[:, 1:3, :], flat_rows[:, 1:3, :], flat_rows[:, 3:5, :], ALU.add))
                then(v.tensor_tensor(flat_rows[:, 2:6:3, :], flat_rows[:, 2:6:3, :], flat_rows[:, 6:8, :], ALU.add))
                if ch == 0:
                    v.wait_ge(over_ready, 2)
                    v.tensor_tensor(over_all[:, :], over_sum[:, 0:1], over_sum[:, 1:2], ALU.add).then_inc(over_added, 1)
                for ty in range(TW):
                    k = ch * TW + ty
                    if ch == 0:
                        v.wait_ge(images_done, {0: 4, 1: 2, 2: 1, 3: 3, 4: 5}[ty])
                    if k >= 3:
                        v.wait_ge(taps_used, k - 2)
                    co = coef[:, :, :, :, :].rearrange("p d k t j -> p (d k) t j")[:, ROW_OF[ty], :, :]
                    img = pbank(IMG0 + ty)
                    spans = window(ch)
                    smin = min(s for s, lo, hi in spans if hi - lo == XC)
                    first_x = ch * XC + smin
                    view = img[:, first_x * C:first_x * C + CH]
                    src = bass.AP(view.tensor, view.offset, [view.ap[0], [C, 3], [GC, XG], [1, GC]])
                    v.tensor_tensor(taps[:, k % 3, smin + 2:smin + 5, :].rearrange("p t (j c) -> p t j c", c=GC),
                                    bcast(co[:, smin + 2:smin + 5, :], 3, GC), src, ALU.mult)
                    for s, lo, hi in spans:
                        if hi - lo == XC:
                            continue
                        x0 = ch * XC + lo + s
                        ins = v.tensor_tensor(taps[:, k % 3, s + 2, lo * C:hi * C].rearrange("p (j c) -> p j c", c=GC),
                                              bcast(co[:, s + 2, lo * G:hi * G], 2, GC),
                                              img[:, x0 * C:(x0 + hi - lo) * C].rearrange("p (j c) -> p j c", c=GC),
                                              ALU.mult)
                    ins.then_inc(taps_ready, 1)
            v.wait_ge(flag_sum, 1)
            v.tensor_scalar(flag[:, :], ps[0:1, 2, 0:1], 0.0, None, ALU.is_gt).then_inc(flag_ready, 1)
            for ch in range(NCH):
                v.wait_ge(taps_used, (ch + 1) * TW)
                ins = v.tensor_tensor(samp[:, ch * CH:(ch + 1) * CH].rearrange("p (j c) -> p j c", c=GC),
                                      pbank(ch, CH).rearrange("p (j c) -> p j c", c=GC),
                                      bcast(rden[:, ch, :], 2, GC), ALU.mult)
            then(ins)
            v.wait_ge(flag_ready, 1)
            far = v.value_load(flag[0:1, 0:1], min_val=0, max_val=1)
            with v.If(far > 0):
                v.wait_ge(img_spread, NI * 16)
                v.wait_ge(late_ready, 3)
                v.tensor_scalar(row_no[:, :], part_no[:, :], NI.bit_length() - 1, None, ALU.logical_shift_right)
                v.drain()
                v.tensor_copy(row_f[:, :], row_no[:, :])
                v.memset(gen_acc[:, :], 0.0)
                v.drain()
                v.tensor_scalar(gen_ky[:, :], coord_ky[:, :], row_f[:, :], None, ALU.add)
                for ch in range(NCH):
                    v.tensor_tensor(gen_x[:, ch, :, :], hat[:, ch, 0:NP, 2, :], hat[:, ch, 0:NP, 0, :], ALU.subtract)
                    v.tensor_tensor(gen_y[:, ch, :, :], hat[:, ch, NP:, 2, :], hat[:, ch, NP:, 0, :], ALU.subtract)
                v.drain()
                for ch in range(NCH):
                    gx = gen_x[:, ch, :, :].rearrange("p s (x g) -> p s x g", g=G)
                    v.tensor_tensor(gx, gx, bcast(coord_x[:, ch, :, :], 3, G), ALU.add)
                    v.tensor_tensor(gen_y[:, ch, :, :], gen_y[:, ch, :, :], bcast(gen_ky[:, :], 2, XG), ALU.add)
                v.drain()

                def nearness(coords, number):
                    v.tensor_scalar(gen_d, coords[:, :, :, :].rearrange("p h s j -> p (h s j)"),
                                    number, 1.0, ALU.subtract, ALU.add)
                    v.drain()
                    v.tensor_scalar(gen_q[:, :], gen_d, -1.0, 2.0, ALU.mult, ALU.add)
                    v.drain()
                    v.tensor_tensor(gen_d, gen_d, gen_q[:, :], ALU.min)
                    v.drain()

                with v.Fori(0, H) as yy:
                    nearness(gen_y, pixel_no[:, bass.ds(yy, 1)])
                    v.scalar_tensor_tensor(out=gen_ey[:, :], in0=gen_d, scalar=0.0,
                                           in1=prob[:, :, :, :, :].rearrange("p h s x g -> p (h s x g)"),
                                           op0=ALU.max, op1=ALU.mult)
                    v.drain()
                    with v.Fori(0, W) as xx:
                        nearness(gen_x, pixel_no[:, bass.ds(xx, 1)])
                        v.scalar_tensor_tensor(out=gen_q[:, :], in0=gen_d, scalar=0.0, in1=gen_ey[:, :],
                                               op0=ALU.max, op1=ALU.mult)
                        v.drain()
                        for ch in range(NCH):
                            v.tensor_reduce(gen_a[:, ch * XG:(ch + 1) * XG],
                                            gen_q[:, ch * NP * XG:(ch + 1) * NP * XG].rearrange("p (s j) -> p j s", s=NP),
                                            AX, ALU.add)
                        v.drain()
                        pixel = image_flat[:, bass.ds(yy * (W * C) + xx * C, C)]
                        v.tensor_tensor(gen_p[:, :].rearrange("p (x g c) -> p x g c", x=W, c=GC),
                                        bcast(gen_a[:, :].rearrange("p (x g) -> p x g", g=G), 3, GC),
                                        bcast(pixel.rearrange("p (g c) -> p g c", c=GC), 1, W), ALU.mult)
                        v.drain()
                        v.tensor_tensor(gen_acc[:, :], gen_acc[:, :], gen_p[:, :], ALU.add)
                        v.drain()
                v.tensor_tensor(samp[:, :].rearrange("p (j c) -> p j c", c=GC),
                                gen_acc[:, :].rearrange("p (j c) -> p j c", c=GC),
                                bcast(rden[:, :, :].rearrange("p h j -> p (h j)"), 2, GC), ALU.mult)
                v.drain()
            v.tensor_copy(samp[:, 0:1], samp[:, 0:1]).then_inc(samp_ready, 1)

            def layer_norm(k, src, dst):
                then(v.tensor_reduce(tok_s[:, :], src, AX, ALU.add))
                then(v.tensor_scalar(tok_s[:, :], tok_s[:, :], 1.0 / C, None, ALU.mult))
                v.tensor_tensor(tok_c[:, :, :], src, bcast(tok_s[:, :], 2, C), ALU.subtract).then_inc(tok_centred, 1)
                v.wait_ge(tok_squared, k)
                then(v.tensor_reduce(tok_v[:, :], tok_q[:, :, :], AX, ALU.add))
                inv_sqrt(tok_r[:, :], tok_v[:, :], 1.0 / C, LN_EPS)
                v.tensor_tensor(dst, tok_c[:, :, :], bcast(tok_r[:, :], 2, C), ALU.mult).then_inc(tok_normed, 1)

            v.wait_ge(conv_out, 1)
            v.wait_ge(x_tok_ready, 1)
            then(v.tensor_tensor(tok[:, :, :].rearrange("p (h n) c -> p h (n c)", h=HALVES),
                                 ps[:, 3:5, 0:NI * C], x_tok[:, :, :, :].rearrange("p h n c -> p h (n c)"), ALU.add))
            layer_norm(1, tok[:, :, :], tok_ln[:, :, :])
            v.wait_ge(pv_done, NI)
            o = ps[:, 3:5, 0:NI * (C + 1)].rearrange("p h (n c) -> p h n c", n=NI)
            then(v.reciprocal(att_r[:, :].rearrange("p (h n) -> p h n", h=HALVES), o[:, :, :, C]))
            for h in range(HALVES):
                ins = v.tensor_tensor(att[:, h * NI:(h + 1) * NI, :], o[:, h, :, 0:C],
                                      bcast(att_r[:, h * NI:(h + 1) * NI], 2, C), ALU.mult)
            then(ins)
            then(v.tensor_tensor(tok2[:, :, :], att[:, :, :], tok[:, :, :], ALU.add))
            layer_norm(2, tok2[:, :, :], tok2_ln[:, :, :])
            v.wait_ge(logits_done, 1)
            v.wait_ge(late_ready, 3)
            then(v.tensor_tensor(logit[:, :, :], pbank(0, NT * NE).rearrange("p (t e) -> p t e", e=NE),
                                 bcast(router_b_all[:, :], 1, NT), ALU.add))

            def pick(src, chosen, m, r):
                then(v.tensor_reduce(top[:, m, :], src, AX, ALU.max))
                then(v.tensor_tensor(lsame[:, :, :], src, bcast(top[:, m, :], 2, NE), ALU.is_equal))
                then(v.tensor_tensor(lsame[:, :, :], lsame[:, :, :], bcast(priority[:, :], 1, NT), ALU.mult))
                then(v.tensor_reduce(top[:, r, :], lsame[:, :, :], AX, ALU.max))
                then(v.tensor_tensor(chosen, lsame[:, :, :], bcast(top[:, r, :], 2, NE), ALU.is_equal))

            pick(logit[:, :, :], first[:, :, :], 0, 1)
            then(v.scalar_tensor_tensor(out=l_rest[:, :, :], in0=first[:, :, :], scalar=OUT_OF_RACE,
                                        in1=logit[:, :, :], op0=ALU.mult, op1=ALU.add))
            pick(l_rest[:, :, :], second[:, :, :], 2, 5)
            v.tensor_tensor(top[:, 3, :], top[:, 2, :], top[:, 0, :], ALU.subtract).then_inc(gap_ready, 1)
            v.wait_ge(gap_exp, 1)
            then(v.tensor_scalar(top[:, 5, :], top[:, 4, :], 1.0, None, ALU.add))
            then(v.reciprocal(top[:, 6, :], top[:, 5, :]))
            v.tensor_tensor(first[:, :, :], first[:, :, :], bcast(top[:, 6, :], 2, NE), ALU.mult)
            then(v.tensor_tensor(top[:, 7, :], top[:, 4, :], top[:, 6, :], ALU.mult))
            then(v.tensor_tensor(second[:, :, :], second[:, :, :], bcast(top[:, 7, :], 2, NE), ALU.mult))
            v.tensor_tensor(gate[:, :, :], first[:, :, :], second[:, :, :], ALU.add).then_inc(gate_ready, 1)
            v.wait_ge(gate_ready, 1)
            for k in range(4):
                i = (k // 2) * NI + (k % 2) * 4
                v.wait_ge(experts_done, k + 1)
                for q in range(4):
                    ins = v.tensor_tensor(gated[:, q, :, :],
                                          pbank(4 - 4 * (k % 2) + q, NE * C).rearrange("p (e c) -> p e c", e=NE),
                                          bcast(gate[:, i + q, :], 2, C), ALU.mult)
                ins.then_inc(experts_read, 1)
                v.wait_ge(experts_read, k + 1)
                then(v.tensor_reduce(moe[:, i:i + 4, :], gated[:, :, :, :].rearrange("p q e c -> p q c e"), AX, ALU.add))
                if k == 0:
                    v.wait_ge(bias_done, 1)
                    v.tensor_tensor(tok2_b[:, :, :], pbank(2).rearrange("p (t c) -> p t c", c=C), tok2[:, :, :],
                                    ALU.add).then_inc(bias_read, 1)
            v.wait_ge(bias_read, 1)
            v.tensor_tensor(result[:, :, :], moe[:, :, :], tok2_b[:, :, :], ALU.add).then_inc(result_ready, 1)

_ARGS = {"x": "x", "L0_conv_w_in": "w_in", "L0_conv_b_in": "b_in", "L0_conv_dw_w": "dw_w",
         "L0_conv_dw_b": "dw_b", "L0_conv_ln_g": "ln_g", "L0_conv_ln_b": "ln_b", "L0_conv_w_off": "w_off",
         "L0_conv_b_off": "b_off", "L0_conv_w_msk": "w_msk", "L0_conv_b_msk": "b_msk",
         "L0_conv_w_out": "w_out", "L0_conv_b_out": "b_out", "L1_ffn_router_w": "router_w",
         "L1_ffn_router_b": "router_b", "L1_ffn_expert_w": "expert_w", "L1_ffn_expert_b": "expert_b"}


def kernel(**inputs):
    import numpy as np
    import concourse.bacc as bacc
    from concourse.bass_utils import run_bass_kernel_spmd as run

    nc = bacc.Bacc("TRN2", target_bir_lowering=False, num_devices=1)
    arrays, aps = {}, {}
    for name, short in _ARGS.items():
        arr = np.ascontiguousarray(inputs[name])
        arrays[f"in_{short}"] = arr
        aps[short] = nc.dram_tensor(f"in_{short}", arr.shape, F32, kind="ExternalInput").ap()
    out = nc.dram_tensor("out_dram", (NI, H, W, C), F32, kind="ExternalOutput").ap()
    hybrid_block(nc, aps, out)
    return run(nc, [arrays], core_ids=[0]).results[0]["out_dram"]
```

```python
from contextlib import ExitStack

import concourse.bass as bass
from concourse import mybir

F32 = mybir.dt.float32
I32 = mybir.dt.int32
ALU = mybir.AluOpType
ACT = mybir.ActivationFunctionType
AX = mybir.AxisListType.X

NI, H, W, C = 8, 16, 16, 32
P = NI * H
G, GC = 8, 4
K = 3
NP = K * K
NOFF, NMSK = 2 * NP * G, NP * G
NPROJ = NOFF + NMSK
PAD = 2 * NI
D = K
TW = 2 * K - 1
CHUNKS = ((0, 4), (4, 8), (12, 4))
MAXG = 8 * G
SLOTS = 5
HALVES = 2
GA = 2
GI = NI // GA
GT = GI * HALVES
NT = NI * HALVES
NE = 8
GN_EPS, CONV_EPS, LN_EPS = 1e-5, 1e-6, 1e-5
SCORE_BOUND = float(C)
MAGIC = 1597463007.0
OUT_OF_RACE = -1e30
WARM = (5, 6, 1, 2, 8, 3, 14, 3, 1, 2, 6, 8, 0, 4, 6, 2)


def bcast(ap, dim, n):
    shape = list(ap.shape)
    return ap.unsqueeze(dim).to_broadcast(shape[:dim] + [n] + shape[dim:])


def window(x0, nx):
    spans = [(s, max(0, -s - x0), min(nx, W - s - x0)) for s in range(1 - K, K)]
    return sorted(spans, key=lambda t: (t[2] - t[1] != nx, t[0]))


def hybrid_block(nc, a, out):
    with ExitStack() as ctx:
        def sb(name, shape, dt=F32):
            return ctx.enter_context(nc.sbuf_tensor(name, shape, dt))

        def sem(name):
            return ctx.enter_context(nc.semaphore(name))

        x_rows = sb("x_rows", [P, W * C])
        x_tok = sb("x_tok", [P, GA, HALVES, GI, C])
        vec_rows = sb("vec_rows", [12, 4, C])
        w_in4 = sb("w_in4", [P, C])
        w_out4 = sb("w_out4", [P, C])
        router4 = sb("router4", [P, NE])
        proj_raw = sb("proj_raw", [97, NPROJ])
        expert4 = sb("expert4", [P, NE, C])
        expert_b8 = sb("expert_b8", [GT * NE, C])
        b_in_row = sb("b_in_row", [1, C])
        b_out_all = sb("b_out_all", [P, C])
        router_b_all = sb("router_b_all", [P, NE])
        wide_ident = sb("wide_ident", [P, P + 2 * PAD])
        ident = wide_ident[:, PAD:PAD + P]
        same_image = sb("same_image", [P, NI])
        seg_mean = sb("seg_mean", [P, P])
        quad_mask = sb("quad_mask", [P, 4])
        tile_mask = sb("tile_mask", [GT * NE, GT])
        ones = sb("ones", [P, P])
        neg_bound = sb("neg_bound", [P, 1])
        minus_one = sb("minus_one", [P, 1])
        eps = sb("eps", [P, 2])
        priority = sb("priority", [P, NE])
        centring = sb("centring", [P, C])
        coord_x = sb("coord_x", [P, W * NP])
        coord_ky = sb("coord_ky", [P, NP])
        pixel_no = sb("pixel_no", [P, W])
        part_no = sb("part_no", [P, 1], I32)
        table = sb("table", [1, 1])
        vec_cols = sb("vec_cols", [P, 12])
        conv_w = sb("conv_w", [P, K, 6, C])
        conv_bias = sb("conv_bias", [P, P])
        w_in_bd = sb("w_in_bd", [P, 4, C])
        w_out_bd = sb("w_out_bd", [P, 4, C])
        router_bd = sb("router_bd", [P, 4, NE])
        proj_mask = sb("proj_mask", [97, 3])
        proj_w = sb("proj_w", [97, 3, NPROJ])
        expert_b_bd = sb("expert_b_bd", [GT * NE, GT, C])
        x_sum = sb("x_sum", [P, C])
        x_cent = sb("x_cent", [P, W * C])
        x_sq = sb("x_sq", [P, W * C])
        x_sqsum = sb("x_sqsum", [P, C])
        gn_std = sb("gn_std", [P, C])
        gn_rstd = sb("gn_rstd", [P, C])
        xnT = sb("xnT", [P, 4, H + 2, NI])
        x_proj = sb("x_proj", [P, W * C])
        c_sq = sb("c_sq", [P, W * C])
        c_sum = sb("c_sum", [P, W])
        c_std = sb("c_std", [P, W])
        c_rstd = sb("c_rstd", [P, W])
        c_norm = sb("c_norm", [P, W * C])
        gT = sb("gT", [97, 6, P])
        l_max = sb("l_max", [P, W * G])
        den = sb("den", [P, W * G])
        rden = sb("rden", [P, W * G])
        prob = sb("prob", [P, NP * W * G])
        absoff = sb("absoff", [P, 2 * NP * MAXG])
        over = sb("over", [P, 2 * NP * MAXG])
        over_sum = sb("over_sum", [P, len(CHUNKS)])
        over_all = sb("over_all", [P, 1])
        flag = sb("flag", [1, 1], I32)
        hat = sb("hat", [P, 2 * NP * D * W * G])
        my = sb("my", [P, 2, D * NP * MAXG])
        coef = sb("coef", [P, 2, D * K * TW * MAXG])
        side1 = sb("side1", [P, 2, D * K * D * MAXG])
        side2 = sb("side2", [P, 2, D * K * MAXG])
        samp = sb("samp", [P, W * C])
        sampT = sb("sampT", [P, NI, H, 4])
        gen_x = sb("gen_x", [P, NP * W * G])
        gen_y = sb("gen_y", [P, NP * W * G])
        gen_ey = sb("gen_ey", [P, NP * W * G])
        gen_d = absoff
        gen_q = over
        gen_p = c_sq
        gen_acc = x_sq
        gen_a = sb("gen_a", [P, W * G])
        gen_ky = sb("gen_ky", [P, NP])
        row_no = sb("row_no", [P, 1], I32)
        row_f = sb("row_f", [P, 1])
        image_all = sb("image_all", [P, H, W * C])
        image_flat = image_all[:, :, :].rearrange("p y j -> p (y j)")
        taps = image_flat[:, 0:SLOTS * TW * MAXG * GC].rearrange("p (k j) -> p k j", k=SLOTS)
        tok = sb("tok", [P, NT, C])
        tok_s = sb("tok_s", [P, NT])
        tok_c = sb("tok_c", [P, NT, C])
        tok_q = sb("tok_q", [P, NT, C])
        tok_v = sb("tok_v", [P, NT])
        tok_d = sb("tok_d", [P, NT])
        tok_r = sb("tok_r", [P, NT])
        tok_ln = sb("tok_ln", [P, NT, C])
        lnT = sb("lnT", [P, GA, HALVES, P])
        probs = image_all[:, 0:H // 2, :].rearrange("p y j -> p (y j)").rearrange(
            "p (n h s) -> p n h s", n=NI, h=HALVES)
        att_d = sb("att_d", [P, NT])
        attT = sb("attT", [P, GA, HALVES * P])
        att_r = sb("att_r", [P, NT])
        tok2 = sb("tok2", [P, NT, C])
        tok2_ln = sb("tok2_ln", [P, NT, C])
        ln2T = sb("ln2T", [P, GA, HALVES, P])
        logit = sb("logit", [P, NT, NE])
        lsame = sb("lsame", [P, NT, NE])
        first = sb("first", [P, NT, NE])
        second = sb("second", [P, NT, NE])
        l_rest = sb("l_rest", [P, NT, NE])
        top = sb("top", [P, 9, NT])
        gate = sb("gate", [P, NT, NE])
        gateT = sb("gateT", [GT * NE, GA, P])
        gated = image_flat[:, NI * HALVES * HALVES * P:][:, 0:GI * HALVES * NE * C].rearrange(
            "p (n h e c) -> p n h e c", n=GI, h=HALVES, e=NE)
        moe = sb("moe", [P, GA, GI * HALVES, C])
        result = sb("result", [P, NT, C])
        nw = sb("nw", [P, 2, GT])

        ps = ctx.enter_context(nc.psum_tensor("ps", [P, 8, 512], F32))
        image_dram = nc.dram_tensor("image_dram", [P, W * C], F32).ap()

        x_in, vec_in, w_in_in, b_in_in, proj_in, tok_in, late_in, img_stored, img_spread, stored = (
            sem(n) for n in ("x_in", "vec_in", "w_in_in", "b_in_in", "proj_in", "tok_in", "late_in",
                             "img_stored", "img_spread", "stored"))
        pool_step, step, table_step = sem("pool_step"), sem("step"), sem("table_step")
        ones_ready, consts, w_in_ready, proj_w_ready, x_tok_ready, late_ready, y_weights_ready, x_weights_ready = (
            sem(n) for n in ("ones_ready", "consts", "w_in_ready", "proj_w_ready", "x_tok_ready", "late_ready",
                             "y_weights_ready", "x_weights_ready"))
        (vec_T, x_mean, x_var, xT_done, conv_done, x_proj_done, conv_T, proj_done, images_done, flag_sum,
         taps_used, sampT_done, conv_out, lnT_done, scores_done, pv_done, att_done, ln2T_done, logits_done,
         gateT_done, bias_done, experts_done) = (
            sem(n) for n in ("vec_T", "x_mean", "x_var", "xT_done", "conv_done", "x_proj_done", "conv_T",
                             "proj_done", "images_done", "flag_sum", "taps_used", "sampT_done", "conv_out",
                             "lnT_done", "scores_done", "pv_done", "att_done", "ln2T_done", "logits_done", "gateT_done",
                             "bias_done", "experts_done"))
        (x_squared, gn_std_ready, conv_squared, conv_std_ready, x_proj_ready, gT_ready, probs_ready, abs_ready,
         hats_ready, over_ready, sampT_ready, tok_squared, tok_std_ready, lnT_ready, exp_done, attT_ready, ln2T_ready,
         tok2_squared, tok2_std_ready, gap_exp, gateT_ready) = (
            sem(n) for n in ("x_squared", "gn_std_ready", "conv_squared", "conv_std_ready", "x_proj_ready",
                             "gT_ready", "probs_ready", "abs_ready", "hats_ready", "over_ready", "sampT_ready",
                             "tok_squared", "tok_std_ready", "lnT_ready", "exp_done", "attT_ready", "ln2T_ready",
                             "tok2_squared", "tok2_std_ready", "gap_exp", "gateT_ready"))
        (seg_ready, conv_w_ready, x_summed, x_centred, x_sqsummed, x_normed, xnT_ready, conv_summed, conv_normed,
         logits_read, over_added, flag_ready, taps_ready, samp_ready, tok_centred, tok_summed, tok_normed,
         tok2_centred, tok2_summed, tok2_normed, gap_ready, gate_ready, experts_read, result_ready) = (
            sem(n) for n in ("seg_ready", "conv_w_ready", "x_summed", "x_centred", "x_sqsummed", "x_normed",
                             "xnT_ready", "conv_summed", "conv_normed", "logits_read", "over_added",
                             "flag_ready", "taps_ready", "samp_ready", "tok_centred", "tok_summed",
                             "tok_normed", "tok2_centred", "tok2_summed", "tok2_normed", "gap_ready",
                             "gate_ready", "experts_read", "result_ready"))

        block = ctx.enter_context(nc.Block())

        def pbank(b, n=512, at=0):
            return ps[:, b, at:at + n]

        proj_ps = ps[:, :, :].rearrange("p b (t j) -> p (b t) j", t=2)
        CHUNK_SLOT = (12, 4, 0)
        IMG0 = 3
        ACC = (2, 0, 1)
        CONV_OUT = PV = 3
        SCORE = (5, 6)
        EXPERT = (7, 0, 5, 6)
        ROW_OF = (0, 1, 2, 5, 8)
        ORDER = ((4, 3, 2, 1, 0), (0, 1, 4, 2, 3), (4, 0, 1, 2, 3))
        IMAGE_ORDER = (3, 4, 2, 1, 0)

        def part(buf, ch, per, pattern, **sizes):
            x0, nx = CHUNKS[ch]
            return buf[:, per * x0 * G:per * (x0 + nx) * G].rearrange(pattern, **sizes)

        def hat_of(ch):
            return part(hat, ch, 2 * NP * D, "p (s d j) -> p s d j", s=2 * NP, d=D)

        def weight_views(ch):
            n = CHUNKS[ch][1] * G
            return (my[:, ch % 2, 0:D * NP * n].rearrange("p (d s j) -> p d s j", d=D, s=NP),
                    coef[:, ch % 2, 0:D * K * TW * n].rearrange("p (r t j) -> p r t j", r=D * K, t=TW),
                    side1[:, ch % 2, 0:D * K * D * n].rearrange("p (r t j) -> p r t j", r=D * K, t=D),
                    side2[:, ch % 2, 0:D * K * n].rearrange("p (r j) -> p r j", r=D * K))

        def y_weights(engine, ch):
            return engine.tensor_tensor(weight_views(ch)[0], bcast(part(prob, ch, NP, "p (s j) -> p s j", s=NP), 1, D),
                                        hat_of(ch)[:, NP:2 * NP, :, :].rearrange("p s d j -> p d s j"), ALU.mult)

        def x_weights(engine, ch, dy):
            weight, rows, s1, s2 = weight_views(ch)
            hats = hat_of(ch)

            def pair(kx, d0, d1):
                return (bcast(weight[:, dy, kx * K:(kx + 1) * K, :], 2, d1 - d0),
                        hats[:, kx * K:(kx + 1) * K, d0:d1, :])

            r = slice(dy * K, (dy + 1) * K)
            engine.tensor_tensor(rows[:, r, 0:3, :], *pair(0, 0, 3), ALU.mult)
            engine.tensor_tensor(s1[:, r, :, :], *pair(1, 0, 3), ALU.mult)
            engine.tensor_tensor(rows[:, r, 3:5, :], *pair(2, 1, 3), ALU.mult)
            return engine.tensor_tensor(s2[:, r, :].unsqueeze(2), *pair(2, 0, 1), ALU.mult)

        def tokens_of(t, ga, h, q2):
            return t.rearrange("n y (b q) c -> q (y b) n c", q=4)[2 * h + q2, :, ga * GI:(ga + 1) * GI, :]

        @block.sync
        def _(sp):
            sp.dma_start(x_rows[:, :], a["x"].rearrange("n y x c -> y n (x c)")).then_inc(x_in, 16)
            sp.dma_start(vec_rows[0:NP, :, :], bcast(a["dw_w"].rearrange("y x o c -> (y x o) c"), 1, 4)).then_inc(vec_in, 16)
            sp.dma_start(w_in4[:, :], a["w_in"].unsqueeze(0).to_broadcast([4, C, C])).then_inc(w_in_in, 16)
            sp.dma_start(proj_raw[0:96, 0:NOFF], a["w_off"].unsqueeze(0).to_broadcast([3, C, NOFF])).then_inc(proj_in, 16)
            sp.dma_start(proj_raw[0:96, NOFF:NPROJ], a["w_msk"].unsqueeze(0).to_broadcast([3, C, NMSK])).then_inc(proj_in, 16)
            sp.dma_start(b_in_row[:, :], a["b_in"].unsqueeze(0)).then_inc(b_in_in, 16)
            sp.dma_start(proj_raw[96:97, 0:NOFF], a["b_off"].unsqueeze(0)).then_inc(proj_in, 16)
            sp.dma_start(proj_raw[96:97, NOFF:NPROJ], a["b_msk"].unsqueeze(0)).then_inc(proj_in, 16)
            sp.dma_start(b_out_all[:, :], a["b_out"].unsqueeze(0).to_broadcast([P, C])).then_inc(tok_in, 16)
            for ga in range(GA):
                for h in range(HALVES):
                    for q2 in range(2):
                        sp.dma_start(x_tok[64 * q2:64 * q2 + 64, ga, h, :, :],
                                     tokens_of(a["x"], ga, h, q2)).then_inc(tok_in, 16)
            for q in range(4):
                sp.dma_start(expert4[q * C:(q + 1) * C, :, :],
                             a["expert_w"].rearrange("e d c -> d e c")).then_inc(late_in, 16)
            sp.dma_start(expert_b8[:, :], a["expert_b"].unsqueeze(0).to_broadcast([GT, NE, C])).then_inc(late_in, 16)
            sp.dma_start(router4[:, :], a["router_w"].unsqueeze(0).to_broadcast([4, C, NE])).then_inc(late_in, 16)
            sp.dma_start(w_out4[:, :], a["w_out"].unsqueeze(0).to_broadcast([4, C, C])).then_inc(late_in, 16)
            sp.dma_start(router_b_all[:, :], a["router_b"].unsqueeze(0).to_broadcast([P, NE])).then_inc(late_in, 16)

            sp.wait_ge(flag_ready, 1)
            far = sp.value_load(flag[0:1, 0:1], min_val=0, max_val=1)
            with sp.If(far > 0):
                sp.wait_ge(x_proj_ready, 1)
                sp.dma_start(image_dram, x_proj[:, :]).then_inc(img_stored, 16)
                sp.wait_ge(img_stored, 16)
                sp.wait_ge(taps_used, len(CHUNKS) * TW)
                for n in range(NI):
                    sp.dma_start(image_all[n:P:NI, :, :],
                                 image_dram[n:P:NI, :].unsqueeze(0).to_broadcast([H, H, W * C])
                                 ).then_inc(img_spread, 16)
            for ga in range(GA):
                sp.wait_ge(result_ready, ga + 1)
                for q2 in range(2):
                    sp.dma_start(tokens_of(out, ga, 0, q2),
                                 result[64 * q2:64 * q2 + 64, ga * GT:ga * GT + GI, :]).then_inc(stored, 16)
            sp.wait_ge(stored, GA * 4 * 16)

        @block.gpsimd
        def _(g):
            count = [0]

            def then(ins):
                count[0] += 1
                ins.then_inc(pool_step, 1)
                g.wait_ge(pool_step, count[0])

            def where(view, pattern, base, mult, op, fill):
                return g.affine_select(out=view, in_=view, compare_op=op, fill=fill, base=base,
                                       pattern=pattern, channel_multiplier=mult)

            g.memset(ones[:, :], 1.0).then_inc(ones_ready, 1)
            then(g.memset(wide_ident[:, :], 0.0))
            where(wide_ident[:, :], [[-1, P + 2 * PAD]], PAD, 1, ALU.not_equal, 1.0).then_inc(consts, 1)
            g.memset(eps[:, 0:1], GN_EPS)
            g.memset(eps[:, 1:2], CONV_EPS)
            g.memset(neg_bound[:, :], -SCORE_BOUND)
            g.memset(minus_one[:, :], -1.0)
            g.memset(conv_w[:, :, :, :], 0.0).then_inc(consts, 1)
            g.memset(xnT[:, :, :, :], 0.0).then_inc(consts, 1)
            then(g.memset(quad_mask[:, :], 1.0))
            then(where(quad_mask[:, :], [[-32, 4]], 0, 1, ALU.is_ge, 0.0))
            then(where(quad_mask[:, :], [[32, 4]], 31, -1, ALU.is_ge, 0.0))
            g.wait_ge(w_in_in, 16)
            g.tensor_tensor(w_in_bd[:, :, :], bcast(w_in4[:, :], 1, 4), bcast(quad_mask[:, :], 2, C),
                            ALU.mult).then_inc(w_in_ready, 1)
            then(g.memset(gT[:, 5, :], 0.0))
            g.memset(gT[96:97, :, :], 1.0).then_inc(consts, 1)
            g.wait_ge(consts, 4)
            then(g.tensor_tensor(proj_mask[:, :], quad_mask[0:97, 0:3],
                                 quad_mask[0:97, 3:4].to_broadcast([97, 3]), ALU.add))
            g.wait_ge(proj_in, 4 * 16)
            for q in range(3):
                g.tensor_scalar(proj_w[:, q, 0:NOFF].rearrange("p (t s g) -> p t s g", t=2, g=G),
                                proj_raw[:, 0:NOFF].rearrange("p (g s t) -> p t s g", g=G, t=2),
                                proj_mask[:, q:q + 1], None, ALU.mult)
                ins = g.tensor_scalar(proj_w[:, q, NOFF:NPROJ].rearrange("p (s g) -> p s g", g=G),
                                      proj_raw[:, NOFF:NPROJ].rearrange("p (g s) -> p s g", g=G),
                                      proj_mask[:, q:q + 1], None, ALU.mult)
            ins.then_inc(proj_w_ready, 1)
            g.wait_ge(tok_in, 9 * 16)
            xt = x_tok[:, :, :, :, :].rearrange("p a h n c -> p (a h n) c")
            g.tensor_tensor(xt, xt, bcast(b_out_all[:, :], 1, NT), ALU.add).then_inc(x_tok_ready, 1)
            g.wait_ge(late_in, 8 * 16)
            g.tensor_tensor(w_out_bd[:, :, :], bcast(w_out4[:, :], 1, 4), bcast(quad_mask[:, :], 2, C),
                            ALU.mult).then_inc(late_ready, 1)
            g.tensor_tensor(router_bd[:, :, :], bcast(router4[:, :], 1, 4), bcast(quad_mask[:, :], 2, NE),
                            ALU.mult).then_inc(late_ready, 1)
            then(g.memset(tile_mask[:, :], 1.0))
            then(where(tile_mask[:, :], [[-NE, GT]], 0, 1, ALU.is_ge, 0.0))
            then(where(tile_mask[:, :], [[NE, GT]], NE - 1, -1, ALU.is_ge, 0.0))
            g.tensor_tensor(expert_b_bd[:, :, :], bcast(expert_b8[:, :], 1, GT),
                            bcast(tile_mask[:, :], 2, C), ALU.mult).then_inc(late_ready, 1)
            g.iota(priority[:, :], [[-1, NE]], base=NE, channel_multiplier=0,
                   allow_small_or_imprecise_dtypes=True)
            for x0, nx in CHUNKS:
                g.iota(coord_x[:, NP * x0:NP * (x0 + nx)].rearrange("p (i j x) -> p i j x", i=K, j=K),
                       [[1, K], [0, K], [1, nx]], base=x0 - 1, channel_multiplier=0,
                       allow_small_or_imprecise_dtypes=True)
            g.iota(coord_ky[:, :], [[0, K], [1, K]], base=-1, channel_multiplier=0,
                   allow_small_or_imprecise_dtypes=True)
            g.iota(part_no[:, :], [[0, 1]], base=0, channel_multiplier=1)
            g.iota(pixel_no[:, :], [[1, W]], base=0, channel_multiplier=0,
                   allow_small_or_imprecise_dtypes=True).then_inc(late_ready, 1)
            for ch in range(1, len(CHUNKS)):
                g.wait_ge(hats_ready, ch + 1)
                g.wait_ge(taps_ready, (ch - 1) * TW + 1)
                y_weights(g, ch).then_inc(y_weights_ready, 1)
            g.wait_ge(y_weights_ready, len(CHUNKS) - 1)
            for dy in range(D):
                ins = x_weights(g, len(CHUNKS) - 1, dy)
            ins.then_inc(x_weights_ready, 1)

        @block.tensor
        def _(pe):
            def keep_warm(bank, n):
                for _ in range(n):
                    pe.matmul(pbank(bank, P), ident, ident, start=True, stop=True)

            pe.wait_ge(consts, 1)
            keep_warm(7, WARM[0])
            pe.wait_ge(seg_ready, 1)
            pe.wait_ge(x_summed, 1)
            pe.matmul(pbank(0, C), seg_mean[:, :], x_sum[:, :], start=True, stop=True).then_inc(x_mean, 1)
            keep_warm(7, WARM[1])
            pe.wait_ge(x_sqsummed, 1)
            pe.matmul(pbank(0, C), seg_mean[:, :], x_sqsum[:, :], start=True, stop=True).then_inc(x_var, 1)
            keep_warm(7, WARM[2])
            pe.wait_ge(vec_in, 4 * 16)
            pe.transpose(pbank(1, 12), vec_rows[:, :, :].rearrange("r q c -> r (q c)"),
                         ident[0:12, 0:12]).then_inc(vec_T, 1)
            keep_warm(7, WARM[3])
            pe.wait_ge(x_normed, 1)
            for b in range(4):
                ins = pe.transpose(pbank(4, P, b * P), x_rows[:, b * P:(b + 1) * P], ident)
            ins.then_inc(xT_done, 1)
            keep_warm(7, WARM[11])
            pe.wait_ge(conv_w_ready, 1)
            pe.matmul(pbank(2), conv_bias[:, :], bcast(centring[:, :], 1, W), start=True, stop=False,
                      skip_group_check=True)
            pe.wait_ge(xnT_ready, 1)
            for b in range(4):
                lo, hi = (1, 6) if b == 0 else (0, 5) if b == 3 else (0, 6)
                x0 = 4 * b - 1 + lo
                for dy in range(K):
                    ins = pe.matmul(pbank(2, (hi - lo) * C, x0 * C),
                                    xnT[:, b, dy:dy + H, :], conv_w[:, dy, lo:hi, :],
                                    start=False, stop=(b == 3 and dy == K - 1), skip_group_check=True)
            ins.then_inc(conv_done, 1)
            pe.wait_ge(b_in_in, 16)
            pe.wait_ge(ones_ready, 1)
            pe.matmul(pbank(3), ones[0:1, :], bcast(b_in_row[:, :], 1, W), start=True, stop=False,
                      skip_group_check=True)
            pe.wait_ge(w_in_ready, 1)
            for b in range(4):
                ins = pe.matmul(pbank(3, P, b * P), xnT[:, b, 1:1 + H, :], w_in_bd[:, :, :],
                                start=False, stop=(b == 3), skip_group_check=True)
            ins.then_inc(x_proj_done, 1)
            keep_warm(7, WARM[4])
            pe.wait_ge(conv_normed, 1)
            for t in range(6):
                n = min(3, W - 3 * t) * C
                bank, at = (0, t * P) if t < 2 else (1, (t - 2) * P)
                ins = pe.transpose(ps[0:n, bank, at:at + P], c_norm[:, 3 * C * t:3 * C * t + n], ident)
                if t in (1, 5):
                    ins.then_inc(conv_T, 1)
            keep_warm(7, WARM[5])
            pe.wait_ge(proj_w_ready, 1)
            for ch, (x0, nx) in enumerate(CHUNKS):
                pe.wait_ge(gT_ready, 1 if ch == 0 else 3)
                if ch == 1:
                    pe.wait_ge(x_proj_ready, 1)
                for i in range(nx):
                    x = x0 + i
                    ins = pe.matmul(proj_ps[:, CHUNK_SLOT[ch] + i, 0:NPROJ], gT[:, x // 3, :],
                                    proj_w[:, x % 3, :], start=True, stop=True)
                ins.then_inc(proj_done, 1)
            for ch, tys in ((0, IMAGE_ORDER[:2]), (1, IMAGE_ORDER[2:])):
                pe.wait_ge(abs_ready, ch + 1)
                pe.wait_ge(hats_ready, ch + 1)
                for ty in tys:
                    at = PAD + NI * (ty - (K - 1))
                    pe.matmul(pbank(IMG0 + ty), wide_ident[:, at:at + P],
                              x_proj[:, :], start=True, stop=True).then_inc(images_done, 1)
            for ch, (x0, nx) in enumerate(CHUNKS):
                if ch == 1:
                    pe.wait_ge(over_added, 1)
                    pe.matmul(ps[0:1, 1, 0:1], over_all[:, :], ones[:, 0:1], start=True, stop=True).then_inc(flag_sum, 1)
                    pe.wait_ge(flag_ready, 1)
                for ty in range(TW):
                    k = ch * TW + ty
                    if ch == 1 and ty < 4:
                        keep_warm(ACC[2], WARM[12 + ty])
                    pe.wait_ge(taps_ready, k + 1)
                    view = taps[:, k % SLOTS, 0:TW * nx * C].rearrange("p (t j) -> p t j", t=TW)
                    for j, (s, lo, hi) in enumerate(window(x0, nx)):
                        ins = pe.matmul(pbank(ACC[ch], (hi - lo) * C, lo * C), ident,
                                        view[:, s + K - 1, lo * C:hi * C],
                                        start=(ty == 0 and j == 0), stop=(ty == TW - 1 and j == TW - 1),
                                        skip_group_check=True)
                    ins.then_inc(taps_used, 1)
            for b in range(4):
                pe.wait_ge(samp_ready, sum(x0 < 4 * (b + 1) for x0, _ in CHUNKS))
                ins = pe.transpose(pbank(7, P, b * P), samp[:, b * P:(b + 1) * P], ident)
            ins.then_inc(sampT_done, 1)
            pe.wait_ge(late_ready, 1)
            for ga in range(GA):
                pe.wait_ge(sampT_ready, ga + 1)
                for h in range(HALVES):
                    for q2 in range(2):
                        for n in range(GI):
                            ins = pe.matmul(ps[64 * q2:64 * q2 + 64, CONV_OUT + ga, (h * GI + n) * C:(h * GI + n + 1) * C],
                                            sampT[:, ga * GI + n, :, :], w_out_bd[:, 2 * h + q2, :],
                                            start=True, stop=True)
                ins.then_inc(conv_out, 1)
            keep_warm(7, WARM[6])

            def channels_first(bank, src, ga):
                for h in range(HALVES):
                    i = ga * GT + h * GI
                    t = pe.transpose(pbank(bank, P, h * P), src[:, i:i + GI, :], ident)
                return t

            def scores(n):
                ga, q = n // GI, n % GI
                if n >= 2:
                    pe.wait_ge(exp_done, n - 1)
                for h in range(HALVES):
                    ins = pe.matmul(pbank(SCORE[n % 2], 2 * P, h * 2 * P), lnT[q * C:(q + 1) * C, ga, h, :],
                                    lnT[q * C:(q + 1) * C, ga, :, :], start=True, stop=True)
                ins.then_inc(scores_done, 1)

            def weighted(n):
                ga, q = n // GI, n % GI
                pe.wait_ge(exp_done, n + 1)
                for h in range(HALVES):
                    ins = pe.matmul(ps[q * C:(q + 1) * C, PV + ga, 0:HALVES * P], tok_ln[:, ga * GT + h * GI + q, :],
                                    probs[:, n, h, :], start=(h == 0), stop=(h == HALVES - 1))
                ins.then_inc(pv_done, 1)

            def att_to_tokens(ga):
                keep_warm(7, WARM[9])
                pe.wait_ge(attT_ready, ga + 1)
                for h in range(HALVES):
                    ins = pe.transpose(pbank(PV + ga, P, (HALVES + h) * P), attT[:, ga, h * P:(h + 1) * P], ident)
                ins.then_inc(att_done, 1)

            def router(ga):
                pe.wait_ge(ln2T_ready, ga + 1)
                pe.wait_ge(late_ready, 4)
                for h in range(HALVES):
                    ins = pe.matmul(pbank(1, GI * NE, h * GI * NE), ln2T[:, ga, h, :], router_bd[:, :, :],
                                    start=True, stop=True)
                ins.then_inc(logits_done, 1)

            def expert_bias(ga):
                pe.wait_ge(gate_ready, ga + 1)
                pe.transpose(ps[0:GT * NE, 1, P:2 * P], gate[:, ga * GT:(ga + 1) * GT, :], ident).then_inc(gateT_done, 1)
                pe.wait_ge(gateT_ready, ga + 1)
                pe.matmul(pbank(PV + ga, GT * C), gateT[:, ga, :], expert_b_bd[:, :, :], start=True,
                          stop=True).then_inc(bias_done, 1)

            def experts(ga):
                for q in range(GI):
                    if ga > 0:
                        pe.wait_ge(experts_read, (ga - 1) * GI + q + 1)
                    for h in range(HALVES):
                        ins = pe.matmul(pbank(EXPERT[q], NE * C, h * NE * C), ln2T[q * C:(q + 1) * C, ga, h, :],
                                        expert4[q * C:(q + 1) * C, :, :], start=True, stop=True)
                    ins.then_inc(experts_done, 1)

            for ga in range(GA):
                pe.wait_ge(tok_normed, ga + 1)
                channels_first(2 - ga, tok_ln, ga).then_inc(lnT_done, 1)
            keep_warm(7, WARM[7])
            pe.wait_ge(lnT_ready, 1)
            scores(0)
            scores(1)
            for n in range(NI):
                keep_warm(7, WARM[8])
                weighted(n)
                if n + 2 < NI:
                    if n + 2 == GI:
                        pe.wait_ge(lnT_ready, 2)
                    scores(n + 2)
                if n == GI - 1:
                    att_to_tokens(0)
            att_to_tokens(1)
            keep_warm(7, WARM[10])
            pe.wait_ge(tok2_normed, 1)
            channels_first(2, tok2_ln, 0).then_inc(ln2T_done, 1)
            router(0)
            experts(0)
            expert_bias(0)
            pe.wait_ge(tok2_normed, 2)
            channels_first(2, tok2_ln, 1).then_inc(ln2T_done, 1)
            router(1)
            experts(1)
            expert_bias(1)

        @block.scalar
        def _(act):
            def load_table(func, done):
                act.activation(table[:, :], ones[0:1, 0:1], func).then_inc(table_step, 1)
                act.wait_ge(table_step, done)

            act.wait_ge(ones_ready, 1)
            load_table(ACT.Sqrt, 1)
            for i, name in enumerate(("dw_b", "ln_g", "ln_b")):
                act.dma_start(vec_rows[NP + i:NP + i + 1, :, :],
                              a[name].unsqueeze(0).unsqueeze(0).to_broadcast([1, 4, C])).then_inc(vec_in, 16)
            act.wait_ge(consts, 2)
            act.wait_ge(x_centred, 1)
            act.activation(x_sq[:, :], x_cent[:, :], ACT.Square).then_inc(x_squared, 1)
            act.wait_ge(x_var, 1)
            act.activation(gn_std[:, :], pbank(0, C), ACT.Sqrt, bias=eps[:, 0:1]).then_inc(gn_std_ready, 1)
            act.wait_ge(consts, 3)
            act.wait_ge(xT_done, 1)
            act.activation(xnT[:, :, 1:1 + H, :], pbank(4).rearrange("p (b y n) -> p b y n", b=4, n=NI),
                           ACT.Copy).then_inc(xnT_ready, 1)
            act.wait_ge(conv_done, 1)
            act.activation(c_sq[:, :], pbank(2), ACT.Square).then_inc(conv_squared, 1)
            act.wait_ge(conv_summed, 1)
            act.activation(c_std[:, :], c_sum[:, :], ACT.Sqrt, bias=eps[:, 1:2], scale=1.0 / C).then_inc(conv_std_ready, 1)
            load_table(ACT.Gelu, 2)
            act.wait_ge(consts, 4)
            act.wait_ge(conv_w_ready, 1)
            for lo, hi, n in ((0, 2, 96), (2, 5, 96), (5, 6, 32)):
                act.wait_ge(conv_T, 1 if lo == 0 else 2)
                at = (lo if lo == 0 else lo - 2) * P
                act.activation(gT[0:n, lo:hi, :].rearrange("p t j -> p (t j)"),
                               ps[0:n, 0 if lo == 0 else 1, at:at + (hi - lo) * P], ACT.Gelu,
                               bias=vec_cols[0:n, 11:12], scale=vec_cols[0:n, 10:11]
                               ).then_inc(gT_ready, 1)
            act.wait_ge(x_proj_done, 1)
            act.activation(x_proj[:, :], pbank(3), ACT.Copy).then_inc(x_proj_ready, 1)
            load_table(ACT.Exp, 3)
            for ch, (x0, nx) in enumerate(CHUNKS):
                slot = CHUNK_SLOT[ch]
                off = proj_ps[:, slot:slot + nx, 0:NOFF].rearrange("p x (s g) -> p x s g", g=G)
                here = hat_of(ch)
                by_x = here.rearrange("p s d (x g) -> p d x s g", g=G)
                ab = absoff[:, 0:2 * NP * nx * G].rearrange("p (s j) -> p s j", s=2 * NP)
                act.wait_ge(logits_read, ch + 1)
                p = part(prob, ch, NP, "p (s j) -> p (s j)", s=NP)
                act.activation(p, p, ACT.Exp).then_inc(probs_ready, 1)
                if ch > 0:
                    act.wait_ge(over_ready, ch)
                act.activation(ab.rearrange("p s (x g) -> p x s g", g=G), off, ACT.Abs).then_inc(abs_ready, 1)
                act.activation(by_x[:, 0], off, ACT.Relu, scale=-1.0)
                act.activation(by_x[:, 2], off, ACT.Relu)
                act.wait_ge(abs_ready, ch + 1)
                act.activation(here[:, :, 1, :], ab, ACT.Copy, bias=1.0, scale=-1.0).then_inc(hats_ready, 1)
                act.activation(over[:, 0:2 * NP * nx * G], absoff[:, 0:2 * NP * nx * G], ACT.Relu,
                               bias=minus_one[:, :], accum_out=over_sum[:, ch:ch + 1]).then_inc(over_ready, 1)
            load_table(ACT.Sqrt, 4)
            act.wait_ge(sampT_done, 1)
            for ga in range(GA):
                act.activation(sampT[:, ga * GI:(ga + 1) * GI, :, :].rearrange("p n y b -> p b y n"),
                               pbank(7).rearrange("p (b y n) -> p b y n", b=4, n=NI)[:, :, :, ga * GI:(ga + 1) * GI],
                               ACT.Copy).then_inc(sampT_ready, 1)

            def squares(ga, centred, squared):
                g = slice(ga * GT, (ga + 1) * GT)
                act.wait_ge(centred, ga + 1)
                act.activation(tok_q[:, g, :], tok_c[:, g, :], ACT.Square).then_inc(squared, 1)

            def deviation(ga, summed, times, ready):
                g = slice(ga * GT, (ga + 1) * GT)
                act.wait_ge(summed, times)
                act.activation(tok_d[:, g], tok_v[:, g], ACT.Sqrt, bias=eps[:, 0:1], scale=1.0 / C).then_inc(ready, 1)

            def exp_scores(n):
                ga, q = n // GI, n % GI
                act.wait_ge(scores_done, n + 1)
                for h in range(HALVES):
                    i = ga * GT + h * GI + q
                    ins = act.activation(probs[:, n, h, :], pbank(SCORE[n % 2], 2 * P, h * 2 * P), ACT.Exp,
                                         bias=neg_bound[:, :], accum_out=att_d[:, i:i + 1])
                ins.then_inc(exp_done, 1)

            def keep_attT(ga):
                act.wait_ge(pv_done, (ga + 1) * GI)
                act.activation(attT[:, ga, :], pbank(PV + ga, HALVES * P), ACT.Copy).then_inc(attT_ready, 1)

            def keep_lnT(dst, ga, bank, done, ready):
                act.wait_ge(done, ga + 1)
                act.activation(dst[:, ga, :, :].rearrange("p h t -> p (h t)"), pbank(bank, 2 * P), ACT.Copy).then_inc(ready, 1)

            def gates(ga):
                g = slice(ga * GT, (ga + 1) * GT)
                act.wait_ge(gap_ready, ga + 1)
                act.activation(top[:, 4, g], top[:, 3, g], ACT.Exp).then_inc(gap_exp, 1)
                act.wait_ge(gateT_done, ga + 1)
                act.activation(gateT[:, ga, :], ps[0:GT * NE, 1, P:2 * P], ACT.Copy).then_inc(gateT_ready, 1)

            squares(0, tok_centred, tok_squared)
            squares(1, tok_centred, tok_squared)
            deviation(0, tok_summed, 1, tok_std_ready)
            deviation(1, tok_summed, 2, tok_std_ready)
            load_table(ACT.Exp, 5)
            keep_lnT(lnT, 0, 2, lnT_done, lnT_ready)
            exp_scores(0)
            keep_lnT(lnT, 1, 1, lnT_done, lnT_ready)
            for n in range(1, GI):
                exp_scores(n)
            keep_attT(0)
            exp_scores(GI)
            exp_scores(GI + 1)
            exp_scores(GI + 2)
            squares(0, tok2_centred, tok2_squared)
            exp_scores(GI + 3)
            keep_attT(1)
            load_table(ACT.Sqrt, 6)
            keep_lnT(ln2T, 0, 2, ln2T_done, ln2T_ready)
            squares(1, tok2_centred, tok2_squared)
            deviation(1, tok2_summed, 1, tok2_std_ready)
            load_table(ACT.Exp, 7)
            gates(0)
            keep_lnT(ln2T, 1, 2, ln2T_done, ln2T_ready)
            gates(1)
            for ga in range(GA):
                act.wait_ge(result_ready, ga + 1)
                for q2 in range(2):
                    act.dma_start(tokens_of(out, ga, 1, q2),
                                  result[64 * q2:64 * q2 + 64, ga * GT + GI:(ga + 1) * GT, :]).then_inc(stored, 16)

        @block.vector
        def _(v):
            count = [0]

            def then(ins):
                count[0] += 1
                ins.then_inc(step, 1)
                v.wait_ge(step, count[0])

            v.wait_ge(consts, 1)
            then(v.tensor_reduce(same_image[:, :], ident.rearrange("p (y n) -> p n y", n=NI), AX, ALU.add))
            v.tensor_scalar(seg_mean[:, :].rearrange("p (y n) -> p y n", n=NI), bcast(same_image[:, :], 1, H),
                            1.0 / (H * W), None, ALU.mult).then_inc(seg_ready, 1)
            then(v.tensor_reduce(centring[:, :], ident.rearrange("p (q c) -> p c q", c=C), AX, ALU.add))
            v.tensor_scalar(centring[:, :], centring[:, :], -1.0 / C, None, ALU.add)
            v.wait_ge(x_in, 16)
            v.tensor_reduce(x_sum[:, :], x_rows[:, :].rearrange("p (x c) -> p c x", c=C), AX,
                            ALU.add).then_inc(x_summed, 1)
            v.wait_ge(x_mean, 1)
            xr = x_rows[:, :].rearrange("p (x c) -> p x c", c=C)
            xc = x_cent[:, :].rearrange("p (x c) -> p x c", c=C)
            v.tensor_tensor(xc, xr, bcast(pbank(0, C), 1, W), ALU.subtract).then_inc(x_centred, 1)
            v.wait_ge(x_squared, 1)
            v.tensor_reduce(x_sqsum[:, :], x_sq[:, :].rearrange("p (x c) -> p c x", c=C), AX,
                            ALU.add).then_inc(x_sqsummed, 1)
            v.wait_ge(gn_std_ready, 1)
            then(v.reciprocal(gn_rstd[:, :], gn_std[:, :]))
            v.tensor_tensor(xr, xc, bcast(gn_rstd[:, :], 1, W), ALU.mult).then_inc(x_normed, 1)
            v.wait_ge(vec_T, 1)
            v.tensor_copy(vec_cols[:, NP:12], pbank(1, 3, NP))
            for dx in range(K):
                ins = v.tensor_copy(vec_cols[:, (K - 1 - dx) * K:(K - dx) * K], ps[:, 1, dx:NP:K])
            then(ins)
            v.wait_ge(consts, 2)
            taps_c = vec_cols[:, 0:NP].rearrange("p (s d) -> p d s", s=K)
            v.tensor_scalar(conv_bias[:, :], ones[:, :], vec_cols[:, 9:10], 0.25, ALU.mult, ALU.mult)

            def tap_weights(xi):
                q = slice(32 * xi, 32 * xi + 32)
                return v.tensor_tensor(conv_w[q, :, xi:xi + K, :],
                                       centring[q, :].unsqueeze(1).unsqueeze(1).to_broadcast([32, K, K, C]),
                                       bcast(taps_c[q, :, :], 3, C), ALU.mult)

            tap_weights(0)
            tap_weights(1)
            tap_weights(2)
            tap_weights(3).then_inc(conv_w_ready, 1)
            v.wait_ge(conv_squared, 1)
            v.tensor_reduce(c_sum[:, :], c_sq[:, :].rearrange("p (x c) -> p x c", c=C), AX, ALU.add).then_inc(conv_summed, 1)
            v.wait_ge(conv_std_ready, 1)
            then(v.reciprocal(c_rstd[:, :], c_std[:, :]))
            v.tensor_tensor(c_norm[:, :].rearrange("p (x c) -> p x c", c=C),
                            pbank(2).rearrange("p (x c) -> p x c", c=C), bcast(c_rstd[:, :], 2, C),
                            ALU.mult).then_inc(conv_normed, 1)

            def mask_logits(ch):
                x0, nx = CHUNKS[ch]
                slot = CHUNK_SLOT[ch]
                v.wait_ge(proj_done, ch + 1)
                logits = proj_ps[:, slot:slot + nx, NOFF:NPROJ]
                lm = l_max[:, x0 * G:(x0 + nx) * G].rearrange("p (x g) -> p x g", g=G)
                then(v.tensor_reduce(lm, logits.rearrange("p x (s g) -> p x g s", g=G), AX, ALU.max))
                v.tensor_tensor(part(prob, ch, NP, "p (s x g) -> p x s g", s=NP, g=G),
                                logits.rearrange("p x (s g) -> p x s g", g=G), bcast(lm, 2, NP),
                                ALU.subtract).then_inc(logits_read, 1)

            def denominators(ch):
                x0, nx = CHUNKS[ch]
                j = slice(x0 * G, (x0 + nx) * G)
                v.wait_ge(probs_ready, ch + 1)
                then(v.tensor_reduce(den[:, j], part(prob, ch, NP, "p (s j) -> p j s", s=NP), AX, ALU.add))
                v.reciprocal(rden[:, j], den[:, j])

            def by_window_column(ch, dys=range(D)):
                _, rows, s1, s2 = weight_views(ch)
                r = slice(dys[0] * K, (dys[-1] + 1) * K)
                then(v.tensor_tensor(rows[:, r, 1:4, :], rows[:, r, 1:4, :], s1[:, r], ALU.add))
                then(v.tensor_tensor(rows[:, r, 2, :], rows[:, r, 2, :], s2[:, r], ALU.add))

            def window_row_1(ch):
                rows = weight_views(ch)[1]
                then(v.tensor_tensor(rows[:, 1], rows[:, 1], rows[:, 3], ALU.add))

            def window_rows_2_3(ch):
                rows = weight_views(ch)[1]
                then(v.tensor_tensor(rows[:, 2], rows[:, 2], rows[:, 4], ALU.add))
                then(v.tensor_tensor(rows[:, 2:6:3], rows[:, 2:6:3], rows[:, 6:8], ALU.add))

            def products(ch, tys):
                x0, nx = CHUNKS[ch]
                rows = weight_views(ch)[1]
                spans = window(x0, nx)
                whole = [s for s, lo, hi in spans if hi - lo == nx]
                for ty in tys:
                    k = ch * TW + ORDER[ch].index(ty)
                    if ch == 0:
                        v.wait_ge(images_done, IMAGE_ORDER.index(ty) + 1)
                    if k >= SLOTS:
                        v.wait_ge(taps_used, k - SLOTS + 1)
                    co = rows[:, ROW_OF[ty], :, :]
                    dst = taps[:, k % SLOTS, 0:TW * nx * C].rearrange("p (t j) -> p t j", t=TW)
                    img = pbank(IMG0 + ty)
                    at = (x0 + whole[0]) * C
                    view = img[:, at:at + nx * C]
                    src = bass.AP(view.tensor, view.offset, [view.ap[0], [C, len(whole)], [GC, nx * G], [1, GC]])
                    t0, t1 = whole[0] + K - 1, whole[-1] + K
                    ins = v.tensor_tensor(dst[:, t0:t1, :].rearrange("p t (j c) -> p t j c", c=GC),
                                          bcast(co[:, t0:t1, :], 3, GC), src, ALU.mult)
                    for s, lo, hi in spans[len(whole):]:
                        at = (x0 + lo + s) * C
                        ins = v.tensor_tensor(dst[:, s + K - 1, lo * C:hi * C].rearrange("p (j c) -> p j c", c=GC),
                                              bcast(co[:, s + K - 1, lo * G:hi * G], 2, GC),
                                              img[:, at:at + (hi - lo) * C].rearrange("p (j c) -> p j c", c=GC),
                                              ALU.mult)
                    ins.then_inc(taps_ready, 1)

            mask_logits(0)
            denominators(0)
            mask_logits(1)
            v.wait_ge(hats_ready, 1)
            then(y_weights(v, 0))
            for dy in range(D):
                ins = x_weights(v, 0, dy)
            then(ins)
            mask_logits(2)
            by_window_column(0)
            window_row_1(0)
            window_rows_2_3(0)
            products(0, ORDER[0])
            denominators(1)
            v.wait_ge(over_ready, len(CHUNKS))
            v.tensor_reduce(over_all[:, :], over_sum[:, :], AX, ALU.add).then_inc(over_added, 1)
            v.wait_ge(y_weights_ready, 1)
            then(x_weights(v, 1, 0))
            by_window_column(1, [0])
            v.wait_ge(flag_sum, 1)
            v.tensor_scalar(flag[:, :], ps[0:1, 1, 0:1], 0.0, None, ALU.is_gt).then_inc(flag_ready, 1)
            products(1, [0])
            then(x_weights(v, 1, 1))
            by_window_column(1, [1])
            window_row_1(1)
            products(1, [1])
            then(x_weights(v, 1, 2))
            by_window_column(1, [2])
            products(1, [4])
            window_rows_2_3(1)
            products(1, [2, 3])
            denominators(2)
            v.wait_ge(x_weights_ready, 1)
            by_window_column(2)
            products(2, [4, 0])
            window_row_1(2)
            window_rows_2_3(2)
            products(2, [1, 2, 3])
            v.wait_ge(flag_ready, 1)
            far = v.value_load(flag[0:1, 0:1], min_val=0, max_val=1)
            with v.If(far > 0):
                v.wait_ge(img_spread, NI * 16)
                v.wait_ge(late_ready, 4)
                v.wait_ge(taps_used, len(CHUNKS) * TW)
                v.tensor_scalar(row_no[:, :], part_no[:, :], NI.bit_length() - 1, None, ALU.logical_shift_right)
                v.drain()
                v.tensor_copy(row_f[:, :], row_no[:, :])
                v.memset(gen_acc[:, :], 0.0)
                v.drain()
                v.tensor_scalar(gen_ky[:, :], coord_ky[:, :], row_f[:, :], None, ALU.add)
                for ch in range(len(CHUNKS)):
                    hats = hat_of(ch)
                    v.tensor_tensor(part(gen_x, ch, NP, "p (s j) -> p s j", s=NP), hats[:, 0:NP, 2, :],
                                    hats[:, 0:NP, 0, :], ALU.subtract)
                    v.tensor_tensor(part(gen_y, ch, NP, "p (s j) -> p s j", s=NP), hats[:, NP:, 2, :],
                                    hats[:, NP:, 0, :], ALU.subtract)
                v.drain()
                for ch, (x0, nx) in enumerate(CHUNKS):
                    gx = part(gen_x, ch, NP, "p (s x g) -> p s x g", s=NP, g=G)
                    gy = part(gen_y, ch, NP, "p (s j) -> p s j", s=NP)
                    cx = coord_x[:, NP * x0:NP * (x0 + nx)].rearrange("p (s x) -> p s x", s=NP)
                    v.tensor_tensor(gx, gx, bcast(cx, 3, G), ALU.add)
                    v.tensor_tensor(gy, gy, bcast(gen_ky[:, :], 2, nx * G), ALU.add)
                v.drain()

                def nearness(coords, number):
                    v.tensor_scalar(gen_d[:, :], coords[:, :], number, 1.0, ALU.subtract, ALU.add)
                    v.drain()
                    v.tensor_scalar(gen_q[:, :], gen_d[:, :], -1.0, 2.0, ALU.mult, ALU.add)
                    v.drain()
                    v.tensor_tensor(gen_d[:, :], gen_d[:, :], gen_q[:, :], ALU.min)
                    v.drain()

                with v.Fori(0, H) as yy:
                    nearness(gen_y, pixel_no[:, bass.ds(yy, 1)])
                    v.scalar_tensor_tensor(out=gen_ey[:, :], in0=gen_d[:, :], scalar=0.0, in1=prob[:, :],
                                           op0=ALU.max, op1=ALU.mult)
                    v.drain()
                    with v.Fori(0, W) as xx:
                        nearness(gen_x, pixel_no[:, bass.ds(xx, 1)])
                        v.scalar_tensor_tensor(out=gen_q[:, :], in0=gen_d[:, :], scalar=0.0, in1=gen_ey[:, :],
                                               op0=ALU.max, op1=ALU.mult)
                        v.drain()
                        for ch, (x0, nx) in enumerate(CHUNKS):
                            v.tensor_reduce(gen_a[:, x0 * G:(x0 + nx) * G],
                                            part(gen_q, ch, NP, "p (s j) -> p j s", s=NP), AX, ALU.add)
                        v.drain()
                        pixel = image_flat[:, bass.ds(yy * (W * C) + xx * C, C)]
                        v.tensor_tensor(gen_p[:, :].rearrange("p (x g c) -> p x g c", x=W, c=GC),
                                        bcast(gen_a[:, :].rearrange("p (x g) -> p x g", g=G), 3, GC),
                                        bcast(pixel.rearrange("p (g c) -> p g c", c=GC), 1, W), ALU.mult)
                        v.drain()
                        v.tensor_tensor(gen_acc[:, :], gen_acc[:, :], gen_p[:, :], ALU.add)
                        v.drain()
                for ch, (x0, nx) in enumerate(CHUNKS):
                    v.tensor_copy(pbank(ACC[ch], nx * C), gen_acc[:, x0 * C:(x0 + nx) * C])
                v.drain()
            for ch, (x0, nx) in enumerate(CHUNKS):
                v.wait_ge(taps_used, (ch + 1) * TW)
                v.tensor_tensor(samp[:, x0 * C:(x0 + nx) * C].rearrange("p (j c) -> p j c", c=GC),
                                      pbank(ACC[ch], nx * C).rearrange("p (j c) -> p j c", c=GC),
                                      bcast(rden[:, x0 * G:(x0 + nx) * G], 2, GC), ALU.mult).then_inc(samp_ready, 1)

            def group(ga):
                return slice(ga * GT, (ga + 1) * GT)

            def centre(ga, src, centred):
                g = group(ga)
                then(v.tensor_reduce(tok_s[:, g], src[:, g, :], AX, ALU.add))
                v.scalar_tensor_tensor(out=tok_c[:, g, :], in0=bcast(tok_s[:, g], 2, C), scalar=-1.0 / C,
                                       in1=src[:, g, :], op0=ALU.mult, op1=ALU.add).then_inc(centred, 1)

            def sum_squares(ga, squared):
                v.wait_ge(squared, ga + 1)
                return v.tensor_reduce(tok_v[:, group(ga)], tok_q[:, group(ga), :], AX, ALU.add)

            def scale(ga, dst, normed):
                g = group(ga)
                v.tensor_tensor(dst[:, g, :], tok_c[:, g, :], bcast(tok_r[:, g], 2, C), ALU.mult).then_inc(normed, 1)

            def by_deviation(ga, dst, ready, times, normed):
                v.wait_ge(ready, times)
                then(v.reciprocal(tok_r[:, group(ga)], tok_d[:, group(ga)]))
                scale(ga, dst, normed)

            def inv_sqrt(y, src, factor, epsilon):
                var, t = nw[:, 0, :], nw[:, 1, :]
                then(v.tensor_scalar(var, src, factor, epsilon, ALU.mult, ALU.add))
                then(v.tensor_scalar(t.bitcast(I32), var.bitcast(I32), 1, None, ALU.logical_shift_right))
                then(v.tensor_scalar(y.bitcast(I32), t.bitcast(I32), -1.0, MAGIC, ALU.mult, ALU.add))
                for _ in range(3):
                    then(v.scalar_tensor_tensor(out=t, in0=y, scalar=-0.5, in1=y, op0=ALU.mult, op1=ALU.mult))
                    then(v.tensor_tensor(t, t, var, ALU.mult))
                    then(v.scalar_tensor_tensor(out=y, in0=t, scalar=1.5, in1=y, op0=ALU.add, op1=ALU.mult))

            v.wait_ge(x_tok_ready, 1)
            for ga in range(GA):
                v.wait_ge(conv_out, ga + 1)
                then(v.tensor_tensor(tok[:, group(ga), :], pbank(CONV_OUT + ga, GT * C).rearrange("p (t c) -> p t c", c=C),
                                     x_tok[:, ga, :, :, :].rearrange("p h n c -> p (h n) c"), ALU.add))
                centre(ga, tok, tok_centred)
            for ga in range(GA):
                sum_squares(ga, tok_squared).then_inc(tok_summed, 1)
            for ga in range(GA):
                by_deviation(ga, tok_ln, tok_std_ready, ga + 1, tok_normed)

            def attended(ga):
                g = group(ga)
                v.wait_ge(exp_done, (ga + 1) * GI)
                then(v.reciprocal(att_r[:, g], att_d[:, g]))
                v.wait_ge(att_done, ga + 1)
                o = pbank(PV + ga, GT * C, HALVES * P).rearrange("p (t c) -> p t c", c=C)
                then(v.tensor_tensor(tok2[:, g, :], o, bcast(att_r[:, g], 2, C), ALU.mult))
                then(v.tensor_tensor(tok2[:, g, :], tok2[:, g, :], tok[:, g, :], ALU.add))
                centre(ga, tok2, tok2_centred)

            def choose(ga):
                g = group(ga)
                v.wait_ge(logits_done, ga + 1)
                v.wait_ge(late_ready, 4)
                then(v.tensor_tensor(logit[:, g, :], pbank(1, GT * NE).rearrange("p (t e) -> p t e", e=NE),
                                     bcast(router_b_all[:, :], 1, GT), ALU.add))

                def pick(src, m, r, chosen):
                    same = lsame[:, g, :]
                    then(v.tensor_reduce(top[:, m, g], src, AX, ALU.max))
                    if m:
                        v.tensor_tensor(top[:, 3, g], top[:, m, g], top[:, 0, g], ALU.subtract).then_inc(gap_ready, 1)
                    then(v.tensor_tensor(same, src, bcast(top[:, m, g], 2, NE), ALU.is_equal))
                    then(v.tensor_tensor(same, same, bcast(priority[:, :], 1, GT), ALU.mult))
                    then(v.tensor_reduce(top[:, r, g], same, AX, ALU.max))
                    then(v.tensor_tensor(chosen, same, bcast(top[:, r, g], 2, NE), ALU.is_equal))

                pick(logit[:, g, :], 0, 1, first[:, g, :])
                then(v.scalar_tensor_tensor(out=l_rest[:, g, :], in0=first[:, g, :], scalar=OUT_OF_RACE,
                                            in1=logit[:, g, :], op0=ALU.mult, op1=ALU.add))
                pick(l_rest[:, g, :], 2, 8, second[:, g, :])
                v.wait_ge(gap_exp, ga + 1)
                then(v.tensor_scalar(top[:, 5, g], top[:, 4, g], 1.0, None, ALU.add))
                then(v.reciprocal(top[:, 6, g], top[:, 5, g]))
                v.tensor_tensor(first[:, g, :], first[:, g, :], bcast(top[:, 6, g], 2, NE), ALU.mult)
                then(v.tensor_tensor(top[:, 7, g], top[:, 4, g], top[:, 6, g], ALU.mult))
                then(v.tensor_tensor(second[:, g, :], second[:, g, :], bcast(top[:, 7, g], 2, NE), ALU.mult))
                v.tensor_tensor(gate[:, g, :], first[:, g, :], second[:, g, :], ALU.add).then_inc(gate_ready, 1)
                v.wait_ge(gate_ready, ga + 1)

            def mixture(ga):
                g = group(ga)
                by_image = gate[:, g, :].rearrange("p (h q) e -> p q h e", h=HALVES)
                for q in range(GI):
                    v.wait_ge(experts_done, ga * GI + q + 1)
                    v.tensor_tensor(gated[:, q, :, :, :], pbank(EXPERT[q]).rearrange("p (h e c) -> p h e c", h=HALVES, e=NE),
                                    bcast(by_image[:, q, :, :], 3, C), ALU.mult).then_inc(experts_read, 1)
                    if q == GI - 1:
                        v.wait_ge(bias_done, ga + 1)
                        v.tensor_tensor(tok2[:, g, :], pbank(PV + ga, GT * C).rearrange("p (t c) -> p t c", c=C),
                                        tok2[:, g, :], ALU.add)
                    if q % 2:
                        v.wait_ge(experts_read, ga * GI + q + 1)
                        ins = v.tensor_reduce(moe[:, ga, (q - 1) * HALVES:(q + 1) * HALVES, :],
                                              gated[:, q - 1:q + 1, :, :, :].rearrange("p q h e c -> p (q h) c e"), AX, ALU.add)
                then(ins)
                v.tensor_tensor(result[:, g, :].rearrange("p (h q) c -> p q h c", h=HALVES),
                                moe[:, ga, :, :].rearrange("p (q h) c -> p q h c", h=HALVES),
                                tok2[:, g, :].rearrange("p (h q) c -> p q h c", h=HALVES), ALU.add).then_inc(result_ready, 1)

            attended(0)
            then(sum_squares(0, tok2_squared))
            inv_sqrt(tok_r[:, group(0)], tok_v[:, group(0)], 1.0 / C, LN_EPS)
            scale(0, tok2_ln, tok2_normed)
            attended(1)
            sum_squares(1, tok2_squared).then_inc(tok2_summed, 1)
            choose(0)
            by_deviation(1, tok2_ln, tok2_std_ready, 1, tok2_normed)
            mixture(0)
            choose(1)
            mixture(1)


_ARGS = {"x": "x", "L0_conv_w_in": "w_in", "L0_conv_b_in": "b_in", "L0_conv_dw_w": "dw_w",
         "L0_conv_dw_b": "dw_b", "L0_conv_ln_g": "ln_g", "L0_conv_ln_b": "ln_b", "L0_conv_w_off": "w_off",
         "L0_conv_b_off": "b_off", "L0_conv_w_msk": "w_msk", "L0_conv_b_msk": "b_msk",
         "L0_conv_w_out": "w_out", "L0_conv_b_out": "b_out", "L1_ffn_router_w": "router_w",
         "L1_ffn_router_b": "router_b", "L1_ffn_expert_w": "expert_w", "L1_ffn_expert_b": "expert_b"}


def kernel(**inputs):
    import numpy as np
    import concourse.bacc as bacc
    from concourse.bass_utils import run_bass_kernel_spmd as run

    nc = bacc.Bacc("TRN2", target_bir_lowering=False, num_devices=1)
    arrays, aps = {}, {}
    for name, short in _ARGS.items():
        arr = np.ascontiguousarray(inputs[name])
        arrays[f"in_{short}"] = arr
        aps[short] = nc.dram_tensor(f"in_{short}", arr.shape, F32, kind="ExternalInput").ap()
    out = nc.dram_tensor("out_dram", (NI, H, W, C), F32, kind="ExternalOutput").ap()
    hybrid_block(nc, aps, out)
    return run(nc, [arrays], core_ids=[0]).results[0]["out_dram"]
```

```python
from contextlib import ExitStack

import concourse.bass as bass
from concourse import mybir

F32 = mybir.dt.float32
I32 = mybir.dt.int32
ALU = mybir.AluOpType
ACT = mybir.ActivationFunctionType
AX = mybir.AxisListType.X

NI, H, W, C = 8, 16, 16, 32
P = NI * H
G, GC = 8, 4
K = 3
NP = K * K
NOFF, NMSK = 2 * NP * G, NP * G
NPROJ = NOFF + NMSK
PAD = 2 * NI
D = K
TW = 2 * K - 1
CHUNKS = ((0, 4), (4, 8), (12, 4))
MAXG = 8 * G
SLOTS = 5
HALVES = 2
GA = 2
GI = NI // GA
GT = GI * HALVES
NT = NI * HALVES
NE = 8
GN_EPS, CONV_EPS, LN_EPS = 1e-5, 1e-6, 1e-5
SCORE_BOUND = float(C)
MAGIC = 1597463007.0
OUT_OF_RACE = -1e30
WARM = {"channel sums": 7, "squares": 7, "vectors": 1, "group norm": 3, "layer norm": 2,
        "projection weights": 1, "token norm": 12, "lnT": 2, "exp": 1, "attT": 2, "second norm": 3,
        "xnT": 6, "window 0": 0, "window 1": 4, "window 2": 3, "window 3": 1,
        "second norm, last group": 6, "ln2T": 2}


def bcast(ap, dim, n):
    shape = list(ap.shape)
    return ap.unsqueeze(dim).to_broadcast(shape[:dim] + [n] + shape[dim:])


def window(x0, nx):
    spans = [(s, max(0, -s - x0), min(nx, W - s - x0)) for s in range(1 - K, K)]
    return sorted(spans, key=lambda t: (t[2] - t[1] != nx, t[0]))


def hybrid_block(nc, a, out):
    with ExitStack() as ctx:
        def sb(name, shape, dt=F32):
            return ctx.enter_context(nc.sbuf_tensor(name, shape, dt))

        def sem(name):
            return ctx.enter_context(nc.semaphore(name))

        x_rows = sb("x_rows", [P, W * C])
        x_tok = sb("x_tok", [P, GA, GI, HALVES, C])
        vec_rows = sb("vec_rows", [12, 4, C])
        w_in4 = sb("w_in4", [P, C])
        w_out4 = sb("w_out4", [P, C])
        router4 = sb("router4", [P, NE])
        proj_raw = sb("proj_raw", [97, NPROJ])
        expert4 = sb("expert4", [P, NE, C])
        expert_b8 = sb("expert_b8", [GT * NE, C])
        b_in_row = sb("b_in_row", [1, C])
        b_out_all = sb("b_out_all", [P, C])
        router_b_row = sb("router_b_row", [1, NE])
        wide_ident = sb("wide_ident", [P, P + 2 * PAD])
        ident = wide_ident[:, PAD:PAD + P]
        same_image = sb("same_image", [P, NI])
        seg_mean = sb("seg_mean", [P, P])
        quad_mask = sb("quad_mask", [P, 4])
        tile_mask = sb("tile_mask", [GT * NE, GT])
        ones = sb("ones", [P, P])
        neg_bound = sb("neg_bound", [P, 1])
        minus_one = sb("minus_one", [P, 1])
        eps = sb("eps", [P, 2])
        priority = sb("priority", [P, NE])
        centring = sb("centring", [P, C])
        coord_x = sb("coord_x", [P, W * NP])
        coord_ky = sb("coord_ky", [P, NP])
        pixel_no = sb("pixel_no", [P, W])
        part_no = sb("part_no", [P, 1], I32)
        table = sb("table", [1, 1])
        vec_cols = sb("vec_cols", [P, 12])
        conv_w = sb("conv_w", [P, K, 6, C])
        conv_bias = sb("conv_bias", [P, P])
        w_in_bd = sb("w_in_bd", [P, 4, C])
        w_out_bd = sb("w_out_bd", [P, 4, C])
        router_bd = sb("router_bd", [P, 4, NE])
        proj_mask = sb("proj_mask", [97, 3])
        proj_w = sb("proj_w", [97, 3, NPROJ])
        expert_b_bd = sb("expert_b_bd", [GT * NE, GT, C])
        x_sum = sb("x_sum", [P, C])
        x_cent = sb("x_cent", [P, W * C])
        x_sq = sb("x_sq", [P, W * C])
        x_sqsum = sb("x_sqsum", [P, C])
        gn_std = sb("gn_std", [P, C])
        gn_rstd = sb("gn_rstd", [P, C])
        xnT = sb("xnT", [P, 4, H + 2, NI])
        x_proj = sb("x_proj", [P, W * C])
        c_sq = sb("c_sq", [P, W * C])
        c_sum = sb("c_sum", [P, W])
        c_std = sb("c_std", [P, W])
        c_rstd = sb("c_rstd", [P, W])
        c_norm = sb("c_norm", [P, W * C])
        gT = sb("gT", [97, 6, P])
        l_max = sb("l_max", [P, W * G])
        den = sb("den", [P, W * G])
        rden = sb("rden", [P, W * G])
        prob = sb("prob", [P, NP * W * G])
        absoff = sb("absoff", [P, 2 * NP * MAXG])
        over = sb("over", [P, 2 * NP * MAXG])
        over_sum = sb("over_sum", [P, len(CHUNKS)])
        over_all = sb("over_all", [P, 1])
        flag = sb("flag", [1, 1], I32)
        hat = sb("hat", [P, 2 * NP * D * W * G])
        my = sb("my", [P, 2, D * NP * MAXG])
        coef = sb("coef", [P, 2, D * K * TW * MAXG])
        side1 = sb("side1", [P, 2, D * K * D * MAXG])
        side2 = sb("side2", [P, 2, D * K * MAXG])
        samp = sb("samp", [P, W * C])
        sampT = sb("sampT", [P, NI, H, 4])
        gen_x = sb("gen_x", [P, NP * W * G])
        gen_y = sb("gen_y", [P, NP * W * G])
        gen_ey = sb("gen_ey", [P, NP * W * G])
        gen_d = absoff
        gen_q = over
        gen_p = c_sq
        gen_acc = x_sq
        gen_a = sb("gen_a", [P, W * G])
        gen_ky = sb("gen_ky", [P, NP])
        row_no = sb("row_no", [P, 1], I32)
        row_f = sb("row_f", [P, 1])
        image_all = sb("image_all", [P, H, W * C])
        image_flat = image_all[:, :, :].rearrange("p y j -> p (y j)")
        taps = image_flat[:, 0:SLOTS * TW * MAXG * GC].rearrange("p (k j) -> p k j", k=SLOTS)
        tok = sb("tok", [P, NT, C])
        tok_s = sb("tok_s", [P, NT])
        tok_c = sb("tok_c", [P, NT, C])
        tok_q = sb("tok_q", [P, NT, C])
        tok_v = sb("tok_v", [P, NT])
        tok_d = sb("tok_d", [P, NT])
        tok_r = sb("tok_r", [P, NT])
        tok_ln = sb("tok_ln", [P, NT, C])
        lnT = sb("lnT", [P, GA, HALVES, P])
        probs = image_all[:, 0:H // 2, :].rearrange("p y j -> p (y j)").rearrange(
            "p (n h s) -> p n h s", n=NI, h=HALVES)
        att_d = sb("att_d", [P, NT])
        attT = sb("attT", [P, GA, HALVES * P])
        att_r = sb("att_r", [P, NT])
        tok2 = sb("tok2", [P, NT, C])
        tok2_ln = sb("tok2_ln", [P, NT, C])
        ln2T = sb("ln2T", [P, GA, HALVES, P])
        lsame = sb("lsame", [P, NT, NE])
        first = sb("first", [P, NT, NE])
        second = sb("second", [P, NT, NE])
        l_rest = sb("l_rest", [P, NT, NE])
        top = sb("top", [P, 6, NT])
        gate = sb("gate", [P, NT, NE])
        gateT = sb("gateT", [GT * NE, GA, P])
        gated = image_flat[:, NI * HALVES * HALVES * P:].rearrange(
            "p (a n h e c) -> p a n h e c", a=GA, n=GI, h=HALVES, e=NE)
        moe = sb("moe", [P, GA, GI, HALVES, C])
        result = sb("result", [P, GA, GI, HALVES, C])
        nw = sb("nw", [P, 2, GT])

        ps = ctx.enter_context(nc.psum_tensor("ps", [P, 8, 512], F32))
        image_dram = nc.dram_tensor("image_dram", [P, W * C], F32).ap()

        x_in, vec_in, w_in_in, b_in_in, proj_in, tok_in, late_in, img_stored, img_spread, stored = (
            sem(n) for n in ("x_in", "vec_in", "w_in_in", "b_in_in", "proj_in", "tok_in", "late_in",
                             "img_stored", "img_spread", "stored"))
        pool_step, step, table_step = sem("pool_step"), sem("step"), sem("table_step")
        ones_ready, consts, w_in_ready, proj_w_ready, x_tok_ready, late_ready, y_weights_ready, x_weights_ready, pair_summed = (
            sem(n) for n in ("ones_ready", "consts", "w_in_ready", "proj_w_ready", "x_tok_ready", "late_ready",
                             "y_weights_ready", "x_weights_ready", "pair_summed"))
        (vec_T, x_mean, x_var, xT_done, conv_done, x_proj_done, conv_T, proj_done, images_done, flag_sum,
         taps_used, sampT_done, conv_out, lnT_done, scores_done, pv_done, att_done, ln2T_done, logits_done,
         gateT_done, experts_done, residual_done) = (
            sem(n) for n in ("vec_T", "x_mean", "x_var", "xT_done", "conv_done", "x_proj_done", "conv_T",
                             "proj_done", "images_done", "flag_sum", "taps_used", "sampT_done", "conv_out",
                             "lnT_done", "scores_done", "pv_done", "att_done", "ln2T_done", "logits_done", "gateT_done",
                             "experts_done", "residual_done"))
        (x_squared, gn_std_ready, xnT_ready, conv_squared, conv_std_ready, x_proj_ready, gT_ready, probs_ready, abs_ready,
         hats_ready, over_ready, sampT_ready, tok_squared, tok_std_ready, exp_done, attT_ready, ln2T_ready,
         tok2_squared, tok2_std_ready, gap_exp, gateT_ready) = (
            sem(n) for n in ("x_squared", "gn_std_ready", "xnT_ready", "conv_squared", "conv_std_ready", "x_proj_ready",
                             "gT_ready", "probs_ready", "abs_ready", "hats_ready", "over_ready", "sampT_ready",
                             "tok_squared", "tok_std_ready", "exp_done", "attT_ready", "ln2T_ready",
                             "tok2_squared", "tok2_std_ready", "gap_exp", "gateT_ready"))
        (seg_ready, conv_w_ready, x_summed, x_centred, x_sqsummed, x_normed, conv_summed, conv_normed,
         logits_read, over_added, flag_ready, taps_ready, samp_ready, tok_centred, tok_summed, tok_normed, lnT_ready,
         tok2_centred, tok2_summed, tok2_normed, gap_ready, gate_ready, gated_ready, result_ready) = (
            sem(n) for n in ("seg_ready", "conv_w_ready", "x_summed", "x_centred", "x_sqsummed", "x_normed",
                             "conv_summed", "conv_normed", "logits_read", "over_added",
                             "flag_ready", "taps_ready", "samp_ready", "tok_centred", "tok_summed",
                             "tok_normed", "lnT_ready", "tok2_centred", "tok2_summed", "tok2_normed", "gap_ready",
                             "gate_ready", "gated_ready", "result_ready"))

        block = ctx.enter_context(nc.Block())

        def pbank(b, n=512, at=0):
            return ps[:, b, at:at + n]

        proj_ps = ps[:, :, :].rearrange("p b (t j) -> p (b t) j", t=2)
        CHUNK_SLOT = (12, 4, 0)
        IMG0 = 3
        ACC = (2, 0, 1)
        CONV_OUT = PV = 3
        SCORE = (5, 6)
        EXPERT = (7, 0, 5, 6)
        ROW_OF = (0, 1, 2, 5, 8)
        ORDER = ((4, 3, 2, 1, 0), (0, 1, 4, 2, 3), (4, 0, 1, 2, 3))
        IMAGE_ORDER = (3, 4, 2, 1, 0)

        def part(buf, ch, per, pattern, **sizes):
            x0, nx = CHUNKS[ch]
            return buf[:, per * x0 * G:per * (x0 + nx) * G].rearrange(pattern, **sizes)

        def hat_of(ch):
            return part(hat, ch, 2 * NP * D, "p (s d j) -> p s d j", s=2 * NP, d=D)

        def weight_views(ch):
            n = CHUNKS[ch][1] * G
            return (my[:, ch % 2, 0:D * NP * n].rearrange("p (d s j) -> p d s j", d=D, s=NP),
                    coef[:, ch % 2, 0:D * K * TW * n].rearrange("p (r t j) -> p r t j", r=D * K, t=TW),
                    side1[:, ch % 2, 0:D * K * D * n].rearrange("p (r t j) -> p r t j", r=D * K, t=D),
                    side2[:, ch % 2, 0:D * K * n].rearrange("p (r j) -> p r j", r=D * K))

        def y_weights(engine, ch):
            return engine.tensor_tensor(weight_views(ch)[0], bcast(part(prob, ch, NP, "p (s j) -> p s j", s=NP), 1, D),
                                        hat_of(ch)[:, NP:2 * NP, :, :].rearrange("p s d j -> p d s j"), ALU.mult)

        def x_weights(engine, ch, dy):
            weight, rows, s1, s2 = weight_views(ch)
            hats = hat_of(ch)

            def pair(kx, d0, d1):
                return (bcast(weight[:, dy, kx * K:(kx + 1) * K, :], 2, d1 - d0),
                        hats[:, kx * K:(kx + 1) * K, d0:d1, :])

            r = slice(dy * K, (dy + 1) * K)
            engine.tensor_tensor(rows[:, r, 0:3, :], *pair(0, 0, 3), ALU.mult)
            engine.tensor_tensor(s1[:, r, :, :], *pair(1, 0, 3), ALU.mult)
            engine.tensor_tensor(rows[:, r, 3:5, :], *pair(2, 1, 3), ALU.mult)
            return engine.tensor_tensor(s2[:, r, :].unsqueeze(2), *pair(2, 0, 1), ALU.mult)

        def tokens_of(t, ga, side):
            return t.rearrange("n y (b s h) c -> s (y b) n (h c)", s=2, h=HALVES)[side, :, ga * GI:(ga + 1) * GI, :]

        def on_chip(buf, ga, side):
            return buf[64 * side:64 * side + 64, ga, :, :, :].rearrange("p n h c -> p n (h c)")

        @block.sync
        def _(sp):
            sp.dma_start(x_rows[:, :], a["x"].rearrange("n y x c -> y n (x c)")).then_inc(x_in, 16)
            sp.dma_start(vec_rows[0:NP, :, :], bcast(a["dw_w"].rearrange("y x o c -> (y x o) c"), 1, 4)).then_inc(vec_in, 16)
            sp.dma_start(w_in4[:, :], a["w_in"].unsqueeze(0).to_broadcast([4, C, C])).then_inc(w_in_in, 16)
            sp.dma_start(proj_raw[0:96, 0:NOFF], a["w_off"].unsqueeze(0).to_broadcast([3, C, NOFF])).then_inc(proj_in, 16)
            sp.dma_start(proj_raw[0:96, NOFF:NPROJ], a["w_msk"].unsqueeze(0).to_broadcast([3, C, NMSK])).then_inc(proj_in, 16)
            sp.dma_start(b_in_row[:, :], a["b_in"].unsqueeze(0)).then_inc(b_in_in, 16)
            sp.dma_start(proj_raw[96:97, 0:NOFF], a["b_off"].unsqueeze(0)).then_inc(proj_in, 16)
            sp.dma_start(proj_raw[96:97, NOFF:NPROJ], a["b_msk"].unsqueeze(0)).then_inc(proj_in, 16)
            sp.dma_start(b_out_all[:, :], a["b_out"].unsqueeze(0).to_broadcast([P, C])).then_inc(tok_in, 16)
            for ga in range(GA):
                for side in range(2):
                    sp.dma_start(on_chip(x_tok, ga, side), tokens_of(a["x"], ga, side)).then_inc(tok_in, 16)
            for q in range(4):
                sp.dma_start(expert4[q * C:(q + 1) * C, :, :],
                             a["expert_w"].rearrange("e d c -> d e c")).then_inc(late_in, 16)
            sp.dma_start(expert_b8[:, :], a["expert_b"].unsqueeze(0).to_broadcast([GT, NE, C])).then_inc(late_in, 16)
            sp.dma_start(router4[:, :], a["router_w"].unsqueeze(0).to_broadcast([4, C, NE])).then_inc(late_in, 16)
            sp.dma_start(w_out4[:, :], a["w_out"].unsqueeze(0).to_broadcast([4, C, C])).then_inc(late_in, 16)
            sp.dma_start(router_b_row[:, :], a["router_b"].unsqueeze(0)).then_inc(late_in, 16)

            sp.wait_ge(flag_ready, 1)
            far = sp.value_load(flag[0:1, 0:1], min_val=0, max_val=1)
            with sp.If(far > 0):
                sp.wait_ge(x_proj_ready, 1)
                sp.dma_start(image_dram, x_proj[:, :]).then_inc(img_stored, 16)
                sp.wait_ge(img_stored, 16)
                sp.wait_ge(taps_used, len(CHUNKS) * TW)
                for n in range(NI):
                    sp.dma_start(image_all[n:P:NI, :, :],
                                 image_dram[n:P:NI, :].unsqueeze(0).to_broadcast([H, H, W * C])
                                 ).then_inc(img_spread, 16)
            sp.wait_ge(result_ready, 1)
            for side in range(2):
                sp.dma_start(tokens_of(out, 0, side), on_chip(result, 0, side)).then_inc(stored, 16)
            sp.wait_ge(result_ready, 2)
            sp.dma_start(tokens_of(out, 1, 0), on_chip(result, 1, 0)).then_inc(stored, 16)
            sp.wait_ge(stored, GA * 2 * 16)

        @block.gpsimd
        def _(g):
            count = [0]

            def then(ins):
                count[0] += 1
                ins.then_inc(pool_step, 1)
                g.wait_ge(pool_step, count[0])

            def where(view, pattern, base, mult, op, fill):
                return g.affine_select(out=view, in_=view, compare_op=op, fill=fill, base=base,
                                       pattern=pattern, channel_multiplier=mult)

            g.memset(ones[:, :], 1.0).then_inc(ones_ready, 1)
            then(g.memset(wide_ident[:, :], 0.0))
            where(wide_ident[:, :], [[-1, P + 2 * PAD]], PAD, 1, ALU.not_equal, 1.0).then_inc(consts, 1)
            g.memset(eps[:, 0:1], GN_EPS)
            g.memset(eps[:, 1:2], CONV_EPS)
            g.memset(neg_bound[:, :], -SCORE_BOUND)
            g.memset(minus_one[:, :], -1.0)
            g.memset(conv_w[:, :, :, :], 0.0).then_inc(consts, 1)
            g.memset(xnT[:, :, :, :], 0.0).then_inc(consts, 1)
            then(g.memset(quad_mask[:, :], 1.0))
            then(where(quad_mask[:, :], [[-32, 4]], 0, 1, ALU.is_ge, 0.0))
            then(where(quad_mask[:, :], [[32, 4]], 31, -1, ALU.is_ge, 0.0))
            g.wait_ge(w_in_in, 16)
            g.tensor_tensor(w_in_bd[:, :, :], bcast(w_in4[:, :], 1, 4), bcast(quad_mask[:, :], 2, C),
                            ALU.mult).then_inc(w_in_ready, 1)
            then(g.memset(gT[:, 5, :], 0.0))
            g.memset(gT[96:97, :, :], 1.0).then_inc(consts, 1)
            g.wait_ge(consts, 4)
            then(g.tensor_tensor(proj_mask[:, :], quad_mask[0:97, 0:3],
                                 quad_mask[0:97, 3:4].to_broadcast([97, 3]), ALU.add))
            g.wait_ge(proj_in, 4 * 16)
            for q in range(3):
                g.tensor_scalar(proj_w[:, q, 0:NOFF].rearrange("p (t s g) -> p t s g", t=2, g=G),
                                proj_raw[:, 0:NOFF].rearrange("p (g s t) -> p t s g", g=G, t=2),
                                proj_mask[:, q:q + 1], None, ALU.mult)
                ins = g.tensor_scalar(proj_w[:, q, NOFF:NPROJ].rearrange("p (s g) -> p s g", g=G),
                                      proj_raw[:, NOFF:NPROJ].rearrange("p (g s) -> p s g", g=G),
                                      proj_mask[:, q:q + 1], None, ALU.mult)
            ins.then_inc(proj_w_ready, 1)
            g.wait_ge(tok_in, 5 * 16)
            xt = x_tok[:, :, :, :, :].rearrange("p a n h c -> p (a n h) c")
            g.tensor_tensor(xt, xt, bcast(b_out_all[:, :], 1, NT), ALU.add).then_inc(x_tok_ready, 1)
            g.wait_ge(late_in, 8 * 16)
            g.tensor_tensor(w_out_bd[:, :, :], bcast(w_out4[:, :], 1, 4), bcast(quad_mask[:, :], 2, C),
                            ALU.mult).then_inc(late_ready, 1)
            g.tensor_tensor(router_bd[:, :, :], bcast(router4[:, :], 1, 4), bcast(quad_mask[:, :], 2, NE),
                            ALU.mult).then_inc(late_ready, 1)
            then(g.memset(tile_mask[:, :], 1.0))
            then(where(tile_mask[:, :], [[-NE, GT]], 0, 1, ALU.is_ge, 0.0))
            then(where(tile_mask[:, :], [[NE, GT]], NE - 1, -1, ALU.is_ge, 0.0))
            g.tensor_tensor(expert_b_bd[:, :, :], bcast(expert_b8[:, :], 1, GT),
                            bcast(tile_mask[:, :], 2, C), ALU.mult).then_inc(late_ready, 1)
            g.iota(priority[:, :], [[-1, NE]], base=NE, channel_multiplier=0,
                   allow_small_or_imprecise_dtypes=True)
            for x0, nx in CHUNKS:
                g.iota(coord_x[:, NP * x0:NP * (x0 + nx)].rearrange("p (i j x) -> p i j x", i=K, j=K),
                       [[1, K], [0, K], [1, nx]], base=x0 - 1, channel_multiplier=0,
                       allow_small_or_imprecise_dtypes=True)
            g.iota(coord_ky[:, :], [[0, K], [1, K]], base=-1, channel_multiplier=0,
                   allow_small_or_imprecise_dtypes=True)
            g.iota(part_no[:, :], [[0, 1]], base=0, channel_multiplier=1)
            g.iota(pixel_no[:, :], [[1, W]], base=0, channel_multiplier=0,
                   allow_small_or_imprecise_dtypes=True).then_inc(late_ready, 1)
            for ch in range(1, len(CHUNKS)):
                g.wait_ge(hats_ready, ch + 1)
                g.wait_ge(taps_ready, (ch - 1) * TW + 1)
                y_weights(g, ch).then_inc(y_weights_ready, 1)
            g.wait_ge(y_weights_ready, len(CHUNKS) - 1)
            for dy in range(D):
                ins = x_weights(g, len(CHUNKS) - 1, dy)
            ins.then_inc(x_weights_ready, 1)
            for pair in range(GA * GI // 2 - 1):
                ga, q = pair // 2, pair % 2 * 2
                g.wait_ge(gated_ready, 2 * pair + 2)
                x = gated[:, ga, q:q + 2, :, :, :].rearrange("p q h e c -> p (q h) (e c)")
                for n in (NE * C // 2, NE * C // 4):
                    then(g.tensor_tensor(x[:, :, 0:n], x[:, :, 0:n], x[:, :, n:2 * n], ALU.add))
                g.tensor_tensor(moe[:, ga, q:q + 2, :, :].rearrange("p q h c -> p (q h) c"), x[:, :, 0:C], x[:, :, C:2 * C],
                                ALU.add).then_inc(pair_summed, 1)

        @block.tensor
        def _(pe):
            def keep_warm(bank, n):
                for _ in range(n):
                    pe.matmul(pbank(bank, P), ident, ident, start=True, stop=True)

            pe.wait_ge(consts, 1)
            keep_warm(7, WARM["channel sums"])
            pe.wait_ge(seg_ready, 1)
            pe.wait_ge(x_summed, 1)
            pe.matmul(pbank(0, C), seg_mean[:, :], x_sum[:, :], start=True, stop=True).then_inc(x_mean, 1)
            keep_warm(7, WARM["squares"])
            pe.wait_ge(x_sqsummed, 1)
            pe.matmul(pbank(0, C), seg_mean[:, :], x_sqsum[:, :], start=True, stop=True).then_inc(x_var, 1)
            keep_warm(7, WARM["vectors"])
            pe.wait_ge(vec_in, 4 * 16)
            pe.transpose(pbank(1, 12), vec_rows[:, :, :].rearrange("r q c -> r (q c)"),
                         ident[0:12, 0:12]).then_inc(vec_T, 1)
            keep_warm(7, WARM["group norm"])
            pe.wait_ge(x_normed, 1)
            for b in range(4):
                ins = pe.transpose(pbank(4, P, b * P), x_rows[:, b * P:(b + 1) * P], ident)
            ins.then_inc(xT_done, 1)
            keep_warm(7, WARM["xnT"])
            pe.wait_ge(conv_w_ready, 1)
            pe.matmul(pbank(2), conv_bias[:, :], bcast(centring[:, :], 1, W), start=True, stop=False,
                      skip_group_check=True)
            pe.wait_ge(xnT_ready, 1)
            for b in range(4):
                lo, hi = (1, 6) if b == 0 else (0, 5) if b == 3 else (0, 6)
                x0 = 4 * b - 1 + lo
                for dy in range(K):
                    ins = pe.matmul(pbank(2, (hi - lo) * C, x0 * C),
                                    xnT[:, b, dy:dy + H, :], conv_w[:, dy, lo:hi, :],
                                    start=False, stop=(b == 3 and dy == K - 1), skip_group_check=True)
            ins.then_inc(conv_done, 1)
            pe.wait_ge(b_in_in, 16)
            pe.wait_ge(ones_ready, 1)
            pe.matmul(pbank(3), ones[0:1, :], bcast(b_in_row[:, :], 1, W), start=True, stop=False,
                      skip_group_check=True)
            pe.wait_ge(w_in_ready, 1)
            for b in range(4):
                ins = pe.matmul(pbank(3, P, b * P), xnT[:, b, 1:1 + H, :], w_in_bd[:, :, :],
                                start=False, stop=(b == 3), skip_group_check=True)
            ins.then_inc(x_proj_done, 1)
            keep_warm(7, WARM["layer norm"])
            pe.wait_ge(conv_normed, 1)
            for t in range(6):
                n = min(3, W - 3 * t) * C
                bank, at = (0, t * P) if t < 2 else (1, (t - 2) * P)
                ins = pe.transpose(ps[0:n, bank, at:at + P], c_norm[:, 3 * C * t:3 * C * t + n], ident)
                if t in (1, 5):
                    ins.then_inc(conv_T, 1)
            keep_warm(7, WARM["projection weights"])
            pe.wait_ge(proj_w_ready, 1)
            for ch, (x0, nx) in enumerate(CHUNKS):
                pe.wait_ge(gT_ready, 1 if ch == 0 else 3)
                if ch == 1:
                    pe.wait_ge(x_proj_ready, 1)
                for i in range(nx):
                    x = x0 + i
                    ins = pe.matmul(proj_ps[:, CHUNK_SLOT[ch] + i, 0:NPROJ], gT[:, x // 3, :],
                                    proj_w[:, x % 3, :], start=True, stop=True)
                ins.then_inc(proj_done, 1)
            for ch, tys in ((0, IMAGE_ORDER[:2]), (1, IMAGE_ORDER[2:])):
                pe.wait_ge(abs_ready, ch + 1)
                pe.wait_ge(hats_ready, ch + 1)
                for ty in tys:
                    at = PAD + NI * (ty - (K - 1))
                    pe.matmul(pbank(IMG0 + ty), wide_ident[:, at:at + P],
                              x_proj[:, :], start=True, stop=True).then_inc(images_done, 1)
            for ch, (x0, nx) in enumerate(CHUNKS):
                if ch == 1:
                    pe.wait_ge(over_added, 1)
                    pe.matmul(ps[0:1, 1, 0:1], over_all[:, :], ones[:, 0:1], start=True, stop=True).then_inc(flag_sum, 1)
                    pe.wait_ge(flag_ready, 1)
                for ty in range(TW):
                    k = ch * TW + ty
                    if ch == 1 and ty < 4:
                        keep_warm(ACC[2], WARM["window %d" % ty])
                    pe.wait_ge(taps_ready, k + 1)
                    view = taps[:, k % SLOTS, 0:TW * nx * C].rearrange("p (t j) -> p t j", t=TW)
                    for j, (s, lo, hi) in enumerate(window(x0, nx)):
                        ins = pe.matmul(pbank(ACC[ch], (hi - lo) * C, lo * C), ident,
                                        view[:, s + K - 1, lo * C:hi * C],
                                        start=(ty == 0 and j == 0), stop=(ty == TW - 1 and j == TW - 1),
                                        skip_group_check=True)
                    ins.then_inc(taps_used, 1)
            for b in range(4):
                pe.wait_ge(samp_ready, sum(x0 < 4 * (b + 1) for x0, _ in CHUNKS))
                ins = pe.transpose(pbank(7, P, b * P), samp[:, b * P:(b + 1) * P], ident)
            ins.then_inc(sampT_done, 1)
            pe.wait_ge(late_ready, 1)
            for ga in range(GA):
                pe.wait_ge(sampT_ready, ga + 1)
                for side in range(2):
                    out_ps = ps[64 * side:64 * side + 64, CONV_OUT + ga, 0:GT * C].rearrange("p (h n c) -> p h n c", h=HALVES, n=GI)
                    for n in range(GI):
                        ins = pe.matmul(out_ps[:, :, n, :], sampT[:, ga * GI + n, :, :],
                                        w_out_bd[:, 2 * side:2 * side + 2, :], start=True, stop=True)
                ins.then_inc(conv_out, 1)
            keep_warm(7, WARM["token norm"])

            def channels_first(bank, src, ga):
                for h in range(HALVES):
                    i = ga * GT + h * GI
                    t = pe.transpose(pbank(bank, P, h * P), src[:, i:i + GI, :], ident)
                return t

            def scores(n):
                ga, q = n // GI, n % GI
                if n >= 2:
                    pe.wait_ge(exp_done, n - 1)
                for h in range(HALVES):
                    ins = pe.matmul(pbank(SCORE[n % 2], 2 * P, h * 2 * P), lnT[q * C:(q + 1) * C, ga, h, :],
                                    lnT[q * C:(q + 1) * C, ga, :, :], start=True, stop=True)
                ins.then_inc(scores_done, 1)

            def weighted(n):
                ga, q = n // GI, n % GI
                pe.wait_ge(exp_done, n + 1)
                for h in range(HALVES):
                    ins = pe.matmul(ps[q * C:(q + 1) * C, PV + ga, 0:HALVES * P], tok_ln[:, ga * GT + h * GI + q, :],
                                    probs[:, n, h, :], start=(h == 0), stop=(h == HALVES - 1))
                ins.then_inc(pv_done, 1)

            def att_to_tokens(ga):
                pe.wait_ge(attT_ready, ga + 1)
                for h in range(HALVES):
                    ins = pe.transpose(pbank(PV + ga, P, (HALVES + h) * P), attT[:, ga, h * P:(h + 1) * P], ident)
                ins.then_inc(att_done, 1)

            def router_bias():
                pe.matmul(pbank(1, GT * NE), ones[0:1, :], bcast(router_b_row[:, :], 1, GT), start=True,
                          stop=False, skip_group_check=True)

            def router(ga):
                pe.wait_ge(ln2T_ready, ga + 1)
                for h in range(HALVES):
                    ins = pe.matmul(pbank(1, GI * NE, h * GI * NE), ln2T[:, ga, h, :], router_bd[:, :, :],
                                    start=False, stop=True, skip_group_check=True)
                ins.then_inc(logits_done, 1)

            def residual(ga):
                g = slice(ga * GT, (ga + 1) * GT)
                total = pbank(PV + ga, GT * C)
                pe.wait_ge(gate_ready, ga + 1)
                pe.transpose(ps[0:GT * NE, PV + ga, 2 * P:3 * P], gate[:, g, :], ident).then_inc(gateT_done, 1)
                pe.wait_ge(gateT_ready, ga + 1)
                pe.matmul(total, gateT[:, ga, :], expert_b_bd[:, :, :], start=True, stop=False)
                pe.matmul(total, ident, tok2[:, g, :], start=False, stop=True).then_inc(residual_done, 1)

            def experts(ga):
                for q in range(GI):
                    if ga > 0:
                        pe.wait_ge(gated_ready, (ga - 1) * GI + q + 1)
                    for h in range(HALVES):
                        ins = pe.matmul(pbank(EXPERT[q], NE * C, h * NE * C), ln2T[q * C:(q + 1) * C, ga, h, :],
                                        expert4[q * C:(q + 1) * C, :, :], start=True, stop=True)
                    ins.then_inc(experts_done, 1)

            for ga in range(GA):
                pe.wait_ge(tok_normed, ga + 1)
                channels_first(2 - ga, tok_ln, ga).then_inc(lnT_done, 1)
            keep_warm(7, WARM["lnT"])
            pe.wait_ge(lnT_ready, 1)
            scores(0)
            scores(1)
            for n in range(NI):
                if n > GI:
                    keep_warm(7, WARM["exp"])
                weighted(n)
                if n + 2 < NI:
                    if n + 2 == GI:
                        pe.wait_ge(lnT_ready, 2)
                    scores(n + 2)
                if n == GI - 1:
                    att_to_tokens(0)
            keep_warm(7, WARM["attT"])
            att_to_tokens(1)
            keep_warm(7, WARM["second norm"])
            pe.wait_ge(late_ready, 4)
            router_bias()
            pe.wait_ge(tok2_normed, 1)
            channels_first(2, tok2_ln, 0).then_inc(ln2T_done, 1)
            router(0)
            experts(0)
            keep_warm(2, WARM["second norm, last group"])
            pe.wait_ge(tok2_normed, 2)
            channels_first(2, tok2_ln, 1).then_inc(ln2T_done, 1)
            keep_warm(PV + 1, WARM["ln2T"])
            router_bias()
            router(1)
            experts(1)
            residual(0)
            residual(1)

        @block.scalar
        def _(act):
            def load_table(func, done):
                act.activation(table[:, :], ones[0:1, 0:1], func).then_inc(table_step, 1)
                act.wait_ge(table_step, done)

            act.wait_ge(ones_ready, 1)
            load_table(ACT.Sqrt, 1)
            for i, name in enumerate(("dw_b", "ln_g", "ln_b")):
                act.dma_start(vec_rows[NP + i:NP + i + 1, :, :],
                              a[name].unsqueeze(0).unsqueeze(0).to_broadcast([1, 4, C])).then_inc(vec_in, 16)
            act.wait_ge(consts, 2)
            act.wait_ge(x_centred, 1)
            act.activation(x_sq[:, :], x_cent[:, :], ACT.Square).then_inc(x_squared, 1)
            act.wait_ge(x_var, 1)
            act.activation(gn_std[:, :], pbank(0, C), ACT.Sqrt, bias=eps[:, 0:1]).then_inc(gn_std_ready, 1)
            act.wait_ge(consts, 3)
            act.wait_ge(xT_done, 1)
            act.activation(xnT[:, :, 1:1 + H, :], pbank(4).rearrange("p (b y n) -> p b y n", b=4, n=NI),
                           ACT.Copy).then_inc(xnT_ready, 1)
            act.wait_ge(conv_done, 1)
            act.activation(c_sq[:, :], pbank(2), ACT.Square).then_inc(conv_squared, 1)
            act.wait_ge(conv_summed, 1)
            act.activation(c_std[:, :], c_sum[:, :], ACT.Sqrt, bias=eps[:, 1:2], scale=1.0 / C).then_inc(conv_std_ready, 1)
            load_table(ACT.Gelu, 2)
            act.wait_ge(consts, 4)
            act.wait_ge(conv_w_ready, 1)
            for lo, hi, n in ((0, 2, 96), (2, 5, 96), (5, 6, 32)):
                act.wait_ge(conv_T, 1 if lo == 0 else 2)
                at = (lo if lo == 0 else lo - 2) * P
                act.activation(gT[0:n, lo:hi, :].rearrange("p t j -> p (t j)"),
                               ps[0:n, 0 if lo == 0 else 1, at:at + (hi - lo) * P], ACT.Gelu,
                               bias=vec_cols[0:n, 11:12], scale=vec_cols[0:n, 10:11]
                               ).then_inc(gT_ready, 1)
            act.wait_ge(x_proj_done, 1)
            act.activation(x_proj[:, :], pbank(3), ACT.Copy).then_inc(x_proj_ready, 1)
            load_table(ACT.Exp, 3)
            for ch, (x0, nx) in enumerate(CHUNKS):
                slot = CHUNK_SLOT[ch]
                off = proj_ps[:, slot:slot + nx, 0:NOFF].rearrange("p x (s g) -> p x s g", g=G)
                here = hat_of(ch)
                by_x = here.rearrange("p s d (x g) -> p d x s g", g=G)
                ab = absoff[:, 0:2 * NP * nx * G].rearrange("p (s j) -> p s j", s=2 * NP)
                act.wait_ge(logits_read, ch + 1)
                p = part(prob, ch, NP, "p (s j) -> p (s j)", s=NP)
                act.activation(p, p, ACT.Exp).then_inc(probs_ready, 1)
                if ch > 0:
                    act.wait_ge(over_ready, ch)
                act.activation(ab.rearrange("p s (x g) -> p x s g", g=G), off, ACT.Abs).then_inc(abs_ready, 1)
                act.activation(by_x[:, 0], off, ACT.Relu, scale=-1.0)
                act.activation(by_x[:, 2], off, ACT.Relu)
                act.wait_ge(abs_ready, ch + 1)
                act.activation(here[:, :, 1, :], ab, ACT.Copy, bias=1.0, scale=-1.0).then_inc(hats_ready, 1)
                act.activation(over[:, 0:2 * NP * nx * G], absoff[:, 0:2 * NP * nx * G], ACT.Relu,
                               bias=minus_one[:, :], accum_out=over_sum[:, ch:ch + 1]).then_inc(over_ready, 1)
            load_table(ACT.Sqrt, 4)
            act.wait_ge(sampT_done, 1)
            for ga in range(GA):
                act.activation(sampT[:, ga * GI:(ga + 1) * GI, :, :].rearrange("p n y b -> p b y n"),
                               pbank(7).rearrange("p (b y n) -> p b y n", b=4, n=NI)[:, :, :, ga * GI:(ga + 1) * GI],
                               ACT.Copy).then_inc(sampT_ready, 1)

            def squares(ga, centred, squared):
                g = slice(ga * GT, (ga + 1) * GT)
                act.wait_ge(centred, ga + 1)
                act.activation(tok_q[:, g, :], tok_c[:, g, :], ACT.Square).then_inc(squared, 1)

            def deviation(ga, summed, times, ready):
                g = slice(ga * GT, (ga + 1) * GT)
                act.wait_ge(summed, times)
                act.activation(tok_d[:, g], tok_v[:, g], ACT.Sqrt, bias=eps[:, 0:1], scale=1.0 / C).then_inc(ready, 1)

            def exp_scores(n):
                ga, q = n // GI, n % GI
                act.wait_ge(scores_done, n + 1)
                for h in range(HALVES):
                    i = ga * GT + h * GI + q
                    ins = act.activation(probs[:, n, h, :], pbank(SCORE[n % 2], 2 * P, h * 2 * P), ACT.Exp,
                                         bias=neg_bound[:, :], accum_out=att_d[:, i:i + 1])
                ins.then_inc(exp_done, 1)

            def keep_ln2T(ga):
                act.wait_ge(ln2T_done, ga + 1)
                act.activation(ln2T[:, ga, :, :].rearrange("p h t -> p (h t)"), pbank(2, 2 * P), ACT.Copy
                               ).then_inc(ln2T_ready, 1)

            def gap_exponential(ga):
                g = slice(ga * GT, (ga + 1) * GT)
                act.wait_ge(gap_ready, ga + 1)
                act.activation(top[:, 2, g], top[:, 1, g], ACT.Exp).then_inc(gap_exp, 1)

            def keep_gateT(ga):
                act.wait_ge(gateT_done, ga + 1)
                act.activation(gateT[:, ga, :], ps[0:GT * NE, PV + ga, 2 * P:3 * P], ACT.Copy).then_inc(gateT_ready, 1)

            squares(0, tok_centred, tok_squared)
            squares(1, tok_centred, tok_squared)
            deviation(0, tok_summed, 1, tok_std_ready)
            deviation(1, tok_summed, 2, tok_std_ready)
            load_table(ACT.Exp, 5)
            exp_scores(0)
            for n in range(1, GI):
                exp_scores(n)
            exp_scores(GI)
            exp_scores(GI + 1)
            squares(0, tok2_centred, tok2_squared)
            exp_scores(GI + 2)
            exp_scores(GI + 3)
            act.wait_ge(pv_done, NI)
            act.activation(attT[:, 1, :], pbank(PV + 1, HALVES * P), ACT.Copy).then_inc(attT_ready, 1)
            load_table(ACT.Sqrt, 6)
            keep_ln2T(0)
            squares(1, tok2_centred, tok2_squared)
            deviation(1, tok2_summed, 1, tok2_std_ready)
            load_table(ACT.Exp, 7)
            gap_exponential(0)
            keep_ln2T(1)
            gap_exponential(1)
            keep_gateT(0)
            keep_gateT(1)
            act.wait_ge(result_ready, 2)
            act.dma_start(tokens_of(out, 1, 1), on_chip(result, 1, 1)).then_inc(stored, 16)

        @block.vector
        def _(v):
            count = [0]

            def then(ins):
                count[0] += 1
                ins.then_inc(step, 1)
                v.wait_ge(step, count[0])

            v.wait_ge(consts, 1)
            then(v.tensor_reduce(same_image[:, :], ident.rearrange("p (y n) -> p n y", n=NI), AX, ALU.add))
            v.tensor_scalar(seg_mean[:, :].rearrange("p (y n) -> p y n", n=NI), bcast(same_image[:, :], 1, H),
                            1.0 / (H * W), None, ALU.mult).then_inc(seg_ready, 1)
            then(v.tensor_reduce(centring[:, :], ident.rearrange("p (q c) -> p c q", c=C), AX, ALU.add))
            v.tensor_scalar(centring[:, :], centring[:, :], -1.0 / C, None, ALU.add)
            v.wait_ge(x_in, 16)
            v.tensor_reduce(x_sum[:, :], x_rows[:, :].rearrange("p (x c) -> p c x", c=C), AX,
                            ALU.add).then_inc(x_summed, 1)
            v.wait_ge(x_mean, 1)
            xr = x_rows[:, :].rearrange("p (x c) -> p x c", c=C)
            xc = x_cent[:, :].rearrange("p (x c) -> p x c", c=C)
            v.tensor_tensor(xc, xr, bcast(pbank(0, C), 1, W), ALU.subtract).then_inc(x_centred, 1)
            v.wait_ge(x_squared, 1)
            v.tensor_reduce(x_sqsum[:, :], x_sq[:, :].rearrange("p (x c) -> p c x", c=C), AX,
                            ALU.add).then_inc(x_sqsummed, 1)
            v.wait_ge(gn_std_ready, 1)
            then(v.reciprocal(gn_rstd[:, :], gn_std[:, :]))
            v.tensor_tensor(xr, xc, bcast(gn_rstd[:, :], 1, W), ALU.mult).then_inc(x_normed, 1)
            v.wait_ge(vec_T, 1)
            v.tensor_copy(vec_cols[:, NP:12], pbank(1, 3, NP))
            for dx in range(K):
                ins = v.tensor_copy(vec_cols[:, (K - 1 - dx) * K:(K - dx) * K], ps[:, 1, dx:NP:K])
            then(ins)
            v.wait_ge(consts, 2)
            taps_c = vec_cols[:, 0:NP].rearrange("p (s d) -> p d s", s=K)
            v.tensor_scalar(conv_bias[:, :], ones[:, :], vec_cols[:, 9:10], 0.25, ALU.mult, ALU.mult)

            def tap_weights(xi):
                q = slice(32 * xi, 32 * xi + 32)
                return v.tensor_tensor(conv_w[q, :, xi:xi + K, :],
                                       centring[q, :].unsqueeze(1).unsqueeze(1).to_broadcast([32, K, K, C]),
                                       bcast(taps_c[q, :, :], 3, C), ALU.mult)

            tap_weights(0)
            tap_weights(1)
            tap_weights(2)
            tap_weights(3).then_inc(conv_w_ready, 1)
            v.wait_ge(conv_squared, 1)
            v.tensor_reduce(c_sum[:, :], c_sq[:, :].rearrange("p (x c) -> p x c", c=C), AX, ALU.add).then_inc(conv_summed, 1)
            v.wait_ge(conv_std_ready, 1)
            then(v.reciprocal(c_rstd[:, :], c_std[:, :]))
            v.tensor_tensor(c_norm[:, :].rearrange("p (x c) -> p x c", c=C),
                            pbank(2).rearrange("p (x c) -> p x c", c=C), bcast(c_rstd[:, :], 2, C),
                            ALU.mult).then_inc(conv_normed, 1)

            def mask_logits(ch):
                x0, nx = CHUNKS[ch]
                slot = CHUNK_SLOT[ch]
                v.wait_ge(proj_done, ch + 1)
                logits = proj_ps[:, slot:slot + nx, NOFF:NPROJ]
                lm = l_max[:, x0 * G:(x0 + nx) * G].rearrange("p (x g) -> p x g", g=G)
                then(v.tensor_reduce(lm, logits.rearrange("p x (s g) -> p x g s", g=G), AX, ALU.max))
                v.tensor_tensor(part(prob, ch, NP, "p (s x g) -> p x s g", s=NP, g=G),
                                logits.rearrange("p x (s g) -> p x s g", g=G), bcast(lm, 2, NP),
                                ALU.subtract).then_inc(logits_read, 1)

            def denominators(ch):
                x0, nx = CHUNKS[ch]
                j = slice(x0 * G, (x0 + nx) * G)
                v.wait_ge(probs_ready, ch + 1)
                then(v.tensor_reduce(den[:, j], part(prob, ch, NP, "p (s j) -> p j s", s=NP), AX, ALU.add))
                v.reciprocal(rden[:, j], den[:, j])

            def by_window_column(ch, dys=range(D)):
                _, rows, s1, s2 = weight_views(ch)
                r = slice(dys[0] * K, (dys[-1] + 1) * K)
                then(v.tensor_tensor(rows[:, r, 1:4, :], rows[:, r, 1:4, :], s1[:, r], ALU.add))
                then(v.tensor_tensor(rows[:, r, 2, :], rows[:, r, 2, :], s2[:, r], ALU.add))

            def window_row_1(ch):
                rows = weight_views(ch)[1]
                then(v.tensor_tensor(rows[:, 1], rows[:, 1], rows[:, 3], ALU.add))

            def window_rows_2_3(ch):
                rows = weight_views(ch)[1]
                then(v.tensor_tensor(rows[:, 2], rows[:, 2], rows[:, 4], ALU.add))
                then(v.tensor_tensor(rows[:, 2:6:3], rows[:, 2:6:3], rows[:, 6:8], ALU.add))

            def products(ch, tys):
                x0, nx = CHUNKS[ch]
                rows = weight_views(ch)[1]
                spans = window(x0, nx)
                whole = [s for s, lo, hi in spans if hi - lo == nx]
                for ty in tys:
                    k = ch * TW + ORDER[ch].index(ty)
                    if ch == 0:
                        v.wait_ge(images_done, IMAGE_ORDER.index(ty) + 1)
                    if k >= SLOTS:
                        v.wait_ge(taps_used, k - SLOTS + 1)
                    co = rows[:, ROW_OF[ty], :, :]
                    dst = taps[:, k % SLOTS, 0:TW * nx * C].rearrange("p (t j) -> p t j", t=TW)
                    img = pbank(IMG0 + ty)
                    at = (x0 + whole[0]) * C
                    view = img[:, at:at + nx * C]
                    src = bass.AP(view.tensor, view.offset, [view.ap[0], [C, len(whole)], [GC, nx * G], [1, GC]])
                    t0, t1 = whole[0] + K - 1, whole[-1] + K
                    ins = v.tensor_tensor(dst[:, t0:t1, :].rearrange("p t (j c) -> p t j c", c=GC),
                                          bcast(co[:, t0:t1, :], 3, GC), src, ALU.mult)
                    for s, lo, hi in spans[len(whole):]:
                        at = (x0 + lo + s) * C
                        ins = v.tensor_tensor(dst[:, s + K - 1, lo * C:hi * C].rearrange("p (j c) -> p j c", c=GC),
                                              bcast(co[:, s + K - 1, lo * G:hi * G], 2, GC),
                                              img[:, at:at + (hi - lo) * C].rearrange("p (j c) -> p j c", c=GC),
                                              ALU.mult)
                    ins.then_inc(taps_ready, 1)

            mask_logits(0)
            denominators(0)
            mask_logits(1)
            v.wait_ge(hats_ready, 1)
            then(y_weights(v, 0))
            for dy in range(D):
                ins = x_weights(v, 0, dy)
            then(ins)
            mask_logits(2)
            by_window_column(0)
            window_row_1(0)
            window_rows_2_3(0)
            products(0, ORDER[0])
            denominators(1)
            v.wait_ge(over_ready, len(CHUNKS))
            v.tensor_reduce(over_all[:, :], over_sum[:, :], AX, ALU.add).then_inc(over_added, 1)
            v.wait_ge(y_weights_ready, 1)
            then(x_weights(v, 1, 0))
            by_window_column(1, [0])
            v.wait_ge(flag_sum, 1)
            v.tensor_scalar(flag[:, :], ps[0:1, 1, 0:1], 0.0, None, ALU.is_gt).then_inc(flag_ready, 1)
            products(1, [0])
            then(x_weights(v, 1, 1))
            by_window_column(1, [1])
            window_row_1(1)
            products(1, [1])
            then(x_weights(v, 1, 2))
            by_window_column(1, [2])
            products(1, [4])
            window_rows_2_3(1)
            products(1, [2, 3])
            denominators(2)
            v.wait_ge(x_weights_ready, 1)
            by_window_column(2)
            products(2, [4, 0])
            window_row_1(2)
            window_rows_2_3(2)
            products(2, [1, 2, 3])
            v.wait_ge(flag_ready, 1)
            far = v.value_load(flag[0:1, 0:1], min_val=0, max_val=1)
            with v.If(far > 0):
                v.wait_ge(img_spread, NI * 16)
                v.wait_ge(late_ready, 4)
                v.wait_ge(taps_used, len(CHUNKS) * TW)
                v.tensor_scalar(row_no[:, :], part_no[:, :], NI.bit_length() - 1, None, ALU.logical_shift_right)
                v.drain()
                v.tensor_copy(row_f[:, :], row_no[:, :])
                v.memset(gen_acc[:, :], 0.0)
                v.drain()
                v.tensor_scalar(gen_ky[:, :], coord_ky[:, :], row_f[:, :], None, ALU.add)
                for ch in range(len(CHUNKS)):
                    hats = hat_of(ch)
                    v.tensor_tensor(part(gen_x, ch, NP, "p (s j) -> p s j", s=NP), hats[:, 0:NP, 2, :],
                                    hats[:, 0:NP, 0, :], ALU.subtract)
                    v.tensor_tensor(part(gen_y, ch, NP, "p (s j) -> p s j", s=NP), hats[:, NP:, 2, :],
                                    hats[:, NP:, 0, :], ALU.subtract)
                v.drain()
                for ch, (x0, nx) in enumerate(CHUNKS):
                    gx = part(gen_x, ch, NP, "p (s x g) -> p s x g", s=NP, g=G)
                    gy = part(gen_y, ch, NP, "p (s j) -> p s j", s=NP)
                    cx = coord_x[:, NP * x0:NP * (x0 + nx)].rearrange("p (s x) -> p s x", s=NP)
                    v.tensor_tensor(gx, gx, bcast(cx, 3, G), ALU.add)
                    v.tensor_tensor(gy, gy, bcast(gen_ky[:, :], 2, nx * G), ALU.add)
                v.drain()

                def nearness(coords, number):
                    v.tensor_scalar(gen_d[:, :], coords[:, :], number, 1.0, ALU.subtract, ALU.add)
                    v.drain()
                    v.tensor_scalar(gen_q[:, :], gen_d[:, :], -1.0, 2.0, ALU.mult, ALU.add)
                    v.drain()
                    v.tensor_tensor(gen_d[:, :], gen_d[:, :], gen_q[:, :], ALU.min)
                    v.drain()

                with v.Fori(0, H) as yy:
                    nearness(gen_y, pixel_no[:, bass.ds(yy, 1)])
                    v.scalar_tensor_tensor(out=gen_ey[:, :], in0=gen_d[:, :], scalar=0.0, in1=prob[:, :],
                                           op0=ALU.max, op1=ALU.mult)
                    v.drain()
                    with v.Fori(0, W) as xx:
                        nearness(gen_x, pixel_no[:, bass.ds(xx, 1)])
                        v.scalar_tensor_tensor(out=gen_q[:, :], in0=gen_d[:, :], scalar=0.0, in1=gen_ey[:, :],
                                               op0=ALU.max, op1=ALU.mult)
                        v.drain()
                        for ch, (x0, nx) in enumerate(CHUNKS):
                            v.tensor_reduce(gen_a[:, x0 * G:(x0 + nx) * G],
                                            part(gen_q, ch, NP, "p (s j) -> p j s", s=NP), AX, ALU.add)
                        v.drain()
                        pixel = image_flat[:, bass.ds(yy * (W * C) + xx * C, C)]
                        v.tensor_tensor(gen_p[:, :].rearrange("p (x g c) -> p x g c", x=W, c=GC),
                                        bcast(gen_a[:, :].rearrange("p (x g) -> p x g", g=G), 3, GC),
                                        bcast(pixel.rearrange("p (g c) -> p g c", c=GC), 1, W), ALU.mult)
                        v.drain()
                        v.tensor_tensor(gen_acc[:, :], gen_acc[:, :], gen_p[:, :], ALU.add)
                        v.drain()
                for ch, (x0, nx) in enumerate(CHUNKS):
                    v.tensor_copy(pbank(ACC[ch], nx * C), gen_acc[:, x0 * C:(x0 + nx) * C])
                v.drain()
            for ch, (x0, nx) in enumerate(CHUNKS):
                v.wait_ge(taps_used, (ch + 1) * TW)
                v.tensor_tensor(samp[:, x0 * C:(x0 + nx) * C].rearrange("p (j c) -> p j c", c=GC),
                                      pbank(ACC[ch], nx * C).rearrange("p (j c) -> p j c", c=GC),
                                      bcast(rden[:, x0 * G:(x0 + nx) * G], 2, GC), ALU.mult).then_inc(samp_ready, 1)

            def group(ga):
                return slice(ga * GT, (ga + 1) * GT)

            def centre(ga, src, centred):
                g = group(ga)
                then(v.tensor_reduce(tok_s[:, g], src[:, g, :], AX, ALU.add))
                v.scalar_tensor_tensor(out=tok_c[:, g, :], in0=bcast(tok_s[:, g], 2, C), scalar=-1.0 / C,
                                       in1=src[:, g, :], op0=ALU.mult, op1=ALU.add).then_inc(centred, 1)

            def sum_squares(ga, squared):
                v.wait_ge(squared, ga + 1)
                return v.tensor_reduce(tok_v[:, group(ga)], tok_q[:, group(ga), :], AX, ALU.add)

            def scale(ga, dst, normed):
                g = group(ga)
                v.tensor_tensor(dst[:, g, :], tok_c[:, g, :], bcast(tok_r[:, g], 2, C), ALU.mult).then_inc(normed, 1)

            def by_deviation(ga, dst, ready, times, normed):
                v.wait_ge(ready, times)
                then(v.reciprocal(tok_r[:, group(ga)], tok_d[:, group(ga)]))
                scale(ga, dst, normed)

            def inv_sqrt(y, src, factor, epsilon):
                var, t = nw[:, 0, :], nw[:, 1, :]
                then(v.tensor_scalar(var, src, factor, epsilon, ALU.mult, ALU.add))
                then(v.tensor_scalar(t.bitcast(I32), var.bitcast(I32), 1, None, ALU.logical_shift_right))
                then(v.tensor_scalar(y.bitcast(I32), t.bitcast(I32), -1.0, MAGIC, ALU.mult, ALU.add))
                for _ in range(3):
                    then(v.scalar_tensor_tensor(out=t, in0=y, scalar=-0.5, in1=y, op0=ALU.mult, op1=ALU.mult))
                    then(v.tensor_tensor(t, t, var, ALU.mult))
                    then(v.scalar_tensor_tensor(out=y, in0=t, scalar=1.5, in1=y, op0=ALU.add, op1=ALU.mult))

            v.wait_ge(x_tok_ready, 1)
            for ga in range(GA):
                v.wait_ge(conv_out, ga + 1)
                then(v.tensor_tensor(tok[:, group(ga), :].rearrange("p (h n) c -> p h n c", h=HALVES),
                                     pbank(CONV_OUT + ga, GT * C).rearrange("p (h n c) -> p h n c", h=HALVES, n=GI),
                                     x_tok[:, ga, :, :, :].rearrange("p n h c -> p h n c"), ALU.add))
                centre(ga, tok, tok_centred)
            for ga in range(GA):
                sum_squares(ga, tok_squared).then_inc(tok_summed, 1)
            for ga in range(GA):
                by_deviation(ga, tok_ln, tok_std_ready, ga + 1, tok_normed)

            for ga in range(GA):
                v.wait_ge(lnT_done, ga + 1)
                v.tensor_copy(lnT[:, ga, :, :].rearrange("p h t -> p (h t)"), pbank(2 - ga, 2 * P)).then_inc(lnT_ready, 1)
            v.wait_ge(pv_done, GI)
            v.tensor_copy(attT[:, 0, :], pbank(PV, HALVES * P)).then_inc(attT_ready, 1)

            def attended(ga):
                g = group(ga)
                v.wait_ge(exp_done, (ga + 1) * GI)
                then(v.reciprocal(att_r[:, g], att_d[:, g]))
                v.wait_ge(att_done, ga + 1)
                o = pbank(PV + ga, GT * C, HALVES * P).rearrange("p (t c) -> p t c", c=C)
                then(v.tensor_tensor(tok2[:, g, :], o, bcast(att_r[:, g], 2, C), ALU.mult))
                then(v.tensor_tensor(tok2[:, g, :], tok2[:, g, :], tok[:, g, :], ALU.add))
                centre(ga, tok2, tok2_centred)

            def choose(ga):
                g = group(ga)
                gap, e, total, rtotal, mark = (top[:, i, g] for i in range(1, 6))
                marks = lsame[:, g, :]
                v.wait_ge(logits_done, ga + 1)
                v.wait_ge(late_ready, 4)
                logit = pbank(1, GT * NE).rearrange("p (t e) -> p t e", e=NE)
                then(v.tensor_reduce(top[:, 0, g], logit, AX, ALU.max))
                then(v.tensor_tensor(l_rest[:, g, :], logit, bcast(top[:, 0, g], 2, NE), ALU.subtract))
                then(v.scalar_tensor_tensor(out=marks, in0=l_rest[:, g, :], scalar=0.0, in1=bcast(priority[:, :], 1, GT),
                                            op0=ALU.is_equal, op1=ALU.mult))
                then(v.tensor_reduce(mark, marks, AX, ALU.max))
                then(v.tensor_tensor(first[:, g, :], marks, bcast(mark, 2, NE), ALU.is_equal))
                then(v.scalar_tensor_tensor(out=l_rest[:, g, :], in0=first[:, g, :], scalar=OUT_OF_RACE,
                                            in1=l_rest[:, g, :], op0=ALU.mult, op1=ALU.add))
                v.tensor_reduce(gap, l_rest[:, g, :], AX, ALU.max).then_inc(gap_ready, 1)
                v.wait_ge(gap_ready, ga + 1)
                then(v.tensor_tensor(marks, l_rest[:, g, :], bcast(gap, 2, NE), ALU.is_equal))
                then(v.tensor_tensor(marks, marks, bcast(priority[:, :], 1, GT), ALU.mult))
                v.tensor_reduce(mark, marks, AX, ALU.max)
                v.wait_ge(gap_exp, ga + 1)
                then(v.tensor_scalar(total, e, 1.0, None, ALU.add))
                v.reciprocal(rtotal, total)
                then(v.tensor_tensor(second[:, g, :], marks, bcast(mark, 2, NE), ALU.is_equal))
                then(v.tensor_tensor(second[:, g, :], second[:, g, :], bcast(e, 2, NE), ALU.mult))
                then(v.tensor_tensor(second[:, g, :], first[:, g, :], second[:, g, :], ALU.add))
                v.tensor_tensor(gate[:, g, :], second[:, g, :], bcast(rtotal, 2, NE), ALU.mult).then_inc(gate_ready, 1)
                v.wait_ge(gate_ready, ga + 1)

            def gated_experts(ga):
                by_image = gate[:, group(ga), :].rearrange("p (h q) e -> p q h e", h=HALVES)
                for q in range(GI):
                    v.wait_ge(experts_done, ga * GI + q + 1)
                    v.tensor_tensor(gated[:, ga, q, :, :, :], pbank(EXPERT[q]).rearrange("p (h e c) -> p h e c", h=HALVES, e=NE),
                                    bcast(by_image[:, q, :, :], 3, C), ALU.mult).then_inc(gated_ready, 1)

            attended(0)
            then(sum_squares(0, tok2_squared))
            inv_sqrt(tok_r[:, group(0)], tok_v[:, group(0)], 1.0 / C, LN_EPS)
            scale(0, tok2_ln, tok2_normed)
            attended(1)
            sum_squares(1, tok2_squared).then_inc(tok2_summed, 1)
            choose(0)
            by_deviation(1, tok2_ln, tok2_std_ready, 1, tok2_normed)
            gated_experts(0)
            choose(1)
            gated_experts(1)
            def finish(ga):
                v.wait_ge(residual_done, ga + 1)
                v.tensor_tensor(result[:, ga].rearrange("p q h c -> p h q c"),
                                pbank(PV + ga, GT * C).rearrange("p (h q c) -> p h q c", h=HALVES, q=GI),
                                moe[:, ga].rearrange("p q h c -> p h q c"), ALU.add).then_inc(result_ready, 1)

            v.wait_ge(pair_summed, 2)
            finish(0)
            v.wait_ge(gated_ready, GA * GI)
            then(v.tensor_reduce(moe[:, 1, 2:4, :, :].rearrange("p q h c -> p (q h) c"),
                                 gated[:, 1, 2:4, :, :, :].rearrange("p q h e c -> p (q h) c e"), AX, ALU.add))
            v.wait_ge(pair_summed, 3)
            finish(1)


_ARGS = {"x": "x", "L0_conv_w_in": "w_in", "L0_conv_b_in": "b_in", "L0_conv_dw_w": "dw_w",
         "L0_conv_dw_b": "dw_b", "L0_conv_ln_g": "ln_g", "L0_conv_ln_b": "ln_b", "L0_conv_w_off": "w_off",
         "L0_conv_b_off": "b_off", "L0_conv_w_msk": "w_msk", "L0_conv_b_msk": "b_msk",
         "L0_conv_w_out": "w_out", "L0_conv_b_out": "b_out", "L1_ffn_router_w": "router_w",
         "L1_ffn_router_b": "router_b", "L1_ffn_expert_w": "expert_w", "L1_ffn_expert_b": "expert_b"}


def kernel(**inputs):
    import numpy as np
    import concourse.bacc as bacc
    from concourse.bass_utils import run_bass_kernel_spmd as run

    nc = bacc.Bacc("TRN2", target_bir_lowering=False, num_devices=1)
    arrays, aps = {}, {}
    for name, short in _ARGS.items():
        arr = np.ascontiguousarray(inputs[name])
        arrays[f"in_{short}"] = arr
        aps[short] = nc.dram_tensor(f"in_{short}", arr.shape, F32, kind="ExternalInput").ap()
    out = nc.dram_tensor("out_dram", (NI, H, W, C), F32, kind="ExternalOutput").ap()
    hybrid_block(nc, aps, out)
    return run(nc, [arrays], core_ids=[0]).results[0]["out_dram"]
```
